# Optimizing a Trainium2 kernel written in Bass

```python
import numpy as np
import jax
import jax.numpy as jnp

def _softmax(x, axis=-1):
    return jax.nn.softmax(x, axis=axis)

def _gelu(x):
    return jax.nn.gelu(x, approximate=True)

def _silu(x):
    return jax.nn.silu(x)

def _sigmoid(x):
    return jax.nn.sigmoid(x)

def _layernorm(x, axis=-1, eps=1e-05):
    m = jnp.mean(x, axis=axis, keepdims=True)
    v = jnp.var(x, axis=axis, keepdims=True)
    return (x - m) / jnp.sqrt(v + eps)

def _scatter_add(tgt, idx, src, axis=0):
    return tgt.at[idx].add(src)

def _segment_sum(src, seg, n):
    return jax.ops.segment_sum(src, seg, n)
kernel_name = 'mk_macaron_d1_jaxref_r2_b2fbbc'

def setup_inputs(seed: int=0):
    np.random.seed(seed)
    _w = jnp.asarray

    def _L0_attn_setup():
        import jax, jax.numpy as jnp
        import numpy as np
        B, S, D, H, DFF = (4, 1024, 512, 16, 2048)
        HD = D // H

        def rmsnorm(x, scale, eps=1e-06):
            var = jnp.mean(jnp.square(x), axis=-1, keepdims=True)
            return x * jax.lax.rsqrt(var + eps) * scale

        def gdn_attention(x, wq, bq, wk, bk, wv, bv, wbeta, bbeta, wo, bo):
            b, s, _ = x.shape
            q = (x @ wq + bq).reshape(b, s, H, HD)
            k = (x @ wk + bk).reshape(b, s, H, HD)
            v = (x @ wv + bv).reshape(b, s, H, HD)
            k = k / (jnp.linalg.norm(k, axis=-1, keepdims=True) + 1e-06)
            beta = jax.nn.sigmoid(x @ wbeta + bbeta)[..., None]
            q = jnp.transpose(q, (1, 0, 2, 3))
            k = jnp.transpose(k, (1, 0, 2, 3))
            v = jnp.transpose(v, (1, 0, 2, 3))
            beta = jnp.transpose(beta, (1, 0, 2, 3))

            def _step(Sm, inputs):
                q_t, k_t, v_t, beta_t = inputs
                Sk = jnp.einsum('bhde,bhe->bhd', Sm, k_t)
                delta = v_t - Sk
                Sm = Sm + beta_t[..., None] * jnp.einsum('bhd,bhe->bhde', delta, k_t)
                o_t = jnp.einsum('bhde,bhe->bhd', Sm, q_t)
                return (Sm, o_t)
            S0 = jnp.zeros((b, H, HD, HD), x.dtype)
            _, outputs = jax.lax.scan(_step, S0, (q, k, v, beta))
            outputs = jnp.transpose(outputs, (1, 0, 2, 3)).reshape(b, s, D)
            return outputs @ wo + bo
        key = jax.random.key(seed)
        ks = jax.random.split(key, 16)
        s = 1.0 / np.sqrt(D)
        inp = {'x': jax.random.normal(ks[0], (B, S, D), jnp.float32), 'wq': jax.random.normal(ks[1], (D, D), jnp.float32) * s, 'bq': jnp.zeros((D,), jnp.float32), 'wk': jax.random.normal(ks[2], (D, D), jnp.float32) * s, 'bk': jnp.zeros((D,), jnp.float32), 'wv': jax.random.normal(ks[3], (D, D), jnp.float32) * s, 'bv': jnp.zeros((D,), jnp.float32), 'wbeta': jax.random.normal(ks[4], (D, H), jnp.float32) * s, 'bbeta': jnp.zeros((H,), jnp.float32), 'wo': jax.random.normal(ks[5], (D, D), jnp.float32) * s, 'bo': jnp.zeros((D,), jnp.float32), 'w1': jax.random.normal(ks[6], (D, DFF), jnp.float32) * s, 'b1': jnp.zeros((DFF,), jnp.float32), 'w2': jax.random.normal(ks[7], (DFF, D), jnp.float32) * (1.0 / np.sqrt(DFF)), 'b2': jnp.zeros((D,), jnp.float32), 'ln1_scale': jnp.ones((D,), jnp.float32), 'ln2_scale': jnp.ones((D,), jnp.float32)}
        return inp
    _L0_attn_in = _L0_attn_setup()

    def _L0_ffn_setup():
        import jax, jax.numpy as jnp
        import numpy as np
        D_MODEL = 512
        M = 64
        INNER = 16
        key = jax.random.key(seed)
        ks = jax.random.split(key, 9)

        def init(k, shape, fan_in):
            bound = 1.0 / np.sqrt(fan_in)
            return jax.random.uniform(k, shape, jnp.float32, -bound, bound)
        x = jax.random.normal(ks[0], (16, 2048, D_MODEL), dtype=jnp.float32)
        Win = init(ks[1], (D_MODEL, M), D_MODEL)
        bin_ = init(ks[2], (M,), D_MODEL)
        W1 = init(ks[3], (M, INNER), 1)
        b1 = init(ks[4], (M, INNER), 1)
        W2 = init(ks[5], (M, INNER), INNER)
        b2 = init(ks[6], (M,), INNER)
        Wout = init(ks[7], (M, D_MODEL), M)
        bout = init(ks[8], (D_MODEL,), M)
        return {'x': x, 'Win': Win, 'bin_': bin_, 'W1': W1, 'b1': b1, 'W2': W2, 'b2': b2, 'Wout': Wout, 'bout': bout}
    _L0_ffn_in = _L0_ffn_setup()
    _d = {'L0_attn_x': _L0_attn_in['x'], 'L0_attn_wq': _L0_attn_in['wq'], 'L0_attn_bq': _L0_attn_in['bq'], 'L0_attn_wk': _L0_attn_in['wk'], 'L0_attn_bk': _L0_attn_in['bk'], 'L0_attn_wv': _L0_attn_in['wv'], 'L0_attn_bv': _L0_attn_in['bv'], 'L0_attn_wbeta': _L0_attn_in['wbeta'], 'L0_attn_bbeta': _L0_attn_in['bbeta'], 'L0_attn_wo': _L0_attn_in['wo'], 'L0_attn_bo': _L0_attn_in['bo'], 'L0_attn_w1': _L0_attn_in['w1'], 'L0_attn_b1': _L0_attn_in['b1'], 'L0_attn_w2': _L0_attn_in['w2'], 'L0_attn_b2': _L0_attn_in['b2'], 'L0_attn_ln1_scale': _L0_attn_in['ln1_scale'], 'L0_attn_ln2_scale': _L0_attn_in['ln2_scale'], 'L0_ffn_Win': _L0_ffn_in['Win'], 'L0_ffn_bin_': _L0_ffn_in['bin_'], 'L0_ffn_W1': _L0_ffn_in['W1'], 'L0_ffn_b1': _L0_ffn_in['b1'], 'L0_ffn_W2': _L0_ffn_in['W2'], 'L0_ffn_b2': _L0_ffn_in['b2'], 'L0_ffn_Wout': _L0_ffn_in['Wout'], 'L0_ffn_bout': _L0_ffn_in['bout']}
    _x0 = _d['L0_attn_x']
    _d['L0_attn_x'] = jax.random.normal(jax.random.fold_in(jax.random.key(seed), 1), (1, 8192, 512), dtype=_x0.dtype)
    del _x0
    return _d

def reference(L0_attn_x, L0_attn_wq, L0_attn_bq, L0_attn_wk, L0_attn_bk, L0_attn_wv, L0_attn_bv, L0_attn_wbeta, L0_attn_bbeta, L0_attn_wo, L0_attn_bo, L0_attn_w1, L0_attn_b1, L0_attn_w2, L0_attn_b2, L0_attn_ln1_scale, L0_attn_ln2_scale, L0_ffn_Win, L0_ffn_bin_, L0_ffn_W1, L0_ffn_b1, L0_ffn_W2, L0_ffn_b2, L0_ffn_Wout, L0_ffn_bout):

    def _L0_attn_ref(x, wq, bq, wk, bk, wv, bv, wbeta, bbeta, wo, bo, w1, b1, w2, b2, ln1_scale, ln2_scale):
        import jax, jax.numpy as jnp
        import numpy as np
        B, S, D, H, DFF = (4, 1024, 512, 16, 2048)
        HD = D // H

        def rmsnorm(x, scale, eps=1e-06):
            var = jnp.mean(jnp.square(x), axis=-1, keepdims=True)
            return x * jax.lax.rsqrt(var + eps) * scale

        def gdn_attention(x, wq, bq, wk, bk, wv, bv, wbeta, bbeta, wo, bo):
            b, s, _ = x.shape
            q = (x @ wq + bq).reshape(b, s, H, HD)
            k = (x @ wk + bk).reshape(b, s, H, HD)
            v = (x @ wv + bv).reshape(b, s, H, HD)
            k = k / (jnp.linalg.norm(k, axis=-1, keepdims=True) + 1e-06)
            beta = jax.nn.sigmoid(x @ wbeta + bbeta)[..., None]
            q = jnp.transpose(q, (1, 0, 2, 3))
            k = jnp.transpose(k, (1, 0, 2, 3))
            v = jnp.transpose(v, (1, 0, 2, 3))
            beta = jnp.transpose(beta, (1, 0, 2, 3))

            def _step(Sm, inputs):
                q_t, k_t, v_t, beta_t = inputs
                Sk = jnp.einsum('bhde,bhe->bhd', Sm, k_t)
                delta = v_t - Sk
                Sm = Sm + beta_t[..., None] * jnp.einsum('bhd,bhe->bhde', delta, k_t)
                o_t = jnp.einsum('bhde,bhe->bhd', Sm, q_t)
                return (Sm, o_t)
            S0 = jnp.zeros((b, H, HD, HD), x.dtype)
            _, outputs = jax.lax.scan(_step, S0, (q, k, v, beta))
            outputs = jnp.transpose(outputs, (1, 0, 2, 3)).reshape(b, s, D)
            return outputs @ wo + bo
        residual = x
        h = rmsnorm(x, ln1_scale)
        h = gdn_attention(h, wq, bq, wk, bk, wv, bv, wbeta, bbeta, wo, bo)
        x = h + residual
        residual = x
        h = rmsnorm(x, ln2_scale)
        h = jax.nn.gelu(h @ w1 + b1) @ w2 + b2
        return h + residual

    def _L0_ffn_ref(x, Win, bin_, W1, b1, W2, b2, Wout, bout):
        import jax, jax.numpy as jnp
        import numpy as np
        D_MODEL = 512
        M = 64
        INNER = 16
        s = jnp.einsum('btd,dm->btm', x, Win) + bin_
        h = jax.nn.relu(s[..., None] * W1 + b1)
        g = jnp.einsum('btmh,mh->btm', h, W2) + b2
        out = jnp.einsum('btm,md->btd', g, Wout) + bout
        return out
    x = L0_attn_x
    x = x + 0.5 * _L0_ffn_ref(_layernorm(x, axis=-1), L0_ffn_Win, L0_ffn_bin_, L0_ffn_W1, L0_ffn_b1, L0_ffn_W2, L0_ffn_b2, L0_ffn_Wout, L0_ffn_bout)
    x = x + _L0_attn_ref(_layernorm(x, axis=-1), L0_attn_wq, L0_attn_bq, L0_attn_wk, L0_attn_bk, L0_attn_wv, L0_attn_bv, L0_attn_wbeta, L0_attn_bbeta, L0_attn_wo, L0_attn_bo, L0_attn_w1, L0_attn_b1, L0_attn_w2, L0_attn_b2, L0_attn_ln1_scale, L0_attn_ln2_scale)
    x = x + 0.5 * _L0_ffn_ref(_layernorm(x, axis=-1), L0_ffn_Win, L0_ffn_bin_, L0_ffn_W1, L0_ffn_b1, L0_ffn_W2, L0_ffn_b2, L0_ffn_Wout, L0_ffn_bout)
    return x

_drawn_inputs = setup_inputs


def setup_inputs(seed=0):
    import zlib

    import numpy as np

    out = dict(_drawn_inputs(seed))
    spreads = {'L0_attn_bq': (0.0, 0.1),
     'L0_attn_bk': (0.0, 0.1),
     'L0_attn_bv': (0.0, 0.1),
     'L0_attn_bbeta': (0.0, 0.284),
     'L0_attn_bo': (0.0, 0.386),
     'L0_attn_b1': (0.0, 0.551),
     'L0_attn_b2': (0.0, 0.358),
     'L0_attn_ln1_scale': (1.0, 0.2),
     'L0_attn_ln2_scale': (1.0, 0.566)}
    factors = {'L0_ffn_bin_': 8.0}
    for name, (base, spread) in spreads.items():
        noise = np.random.default_rng([zlib.crc32(name.encode()), seed]).standard_normal(out[name].shape)
        drawn = base * np.exp(spread * noise) if base else spread * noise
        out[name] = jnp.asarray(drawn.astype(out[name].dtype))
    for name, factor in factors.items():
        out[name] = (out[name] * factor).astype(out[name].dtype)
    return out
```

```python
from contextlib import ExitStack

import concourse.bass as bass
import concourse.mybir as mybir
import numpy as np

F32 = mybir.dt.float32
F32R = mybir.dt.float32r
ALU = mybir.AluOpType
ACT = mybir.ActivationFunctionType
AX = mybir.AxisListType

P = 128
D = 512
NF = D // P
HEADS, HD = 16, 32
GROUPS = HEADS // 4
DFF = 2048
NM = DFF // P
TOK = 512
NB = TOK // P
SUP = 1024
CH = 32
NC = SUP // CH
NU = GROUPS * NC
LN_EPS, RMS_EPS, NORM_EPS = 1e-5, 1e-6, 1e-6

SHORT = {"allow_slow_non_contiguous": True}

C_ID, C_GM, C_BD, C_EYE, C_POW, C_END = 0, 128, 192, 196, 228, 244


def shape_constants():
    c = np.zeros((P, C_END), np.float32)
    p = np.arange(P)
    j = (p % CH)[:, None]
    i = np.arange(CH)[None, :]
    c[:, C_ID:C_GM] = np.eye(P)
    c[:, C_GM:C_GM + 32] = -1.0 * (j < i)
    c[:, C_GM + 32:C_BD] = j <= i
    c[:, C_BD:C_EYE] = (p // 32)[:, None] == np.arange(4)
    c[:, C_EYE:C_POW] = j == i
    c[:, C_POW:C_POW + 8] = -0.5
    c[:, C_POW + 8:C_END] = 0.5
    return c


class Lane:

    def __init__(self, sem):
        self.sem, self.count, self.work, self.waited = sem, 0, [], {}

    def do(self, issue, *waits):
        self.wait(*waits)
        self.count += 1
        self.work.append(("do", issue, None))
        return self.sem, self.count

    def wait(self, *waits):
        for w in waits:
            if w is None:
                continue
            if isinstance(w, list):
                self.wait(*w)
                continue
            sem, value = w
            if self.waited.get(id(sem), 0) < value:
                self.waited[id(sem)] = value
                self.work.append(("wait", sem, value))

    def dma(self, box, out, src, *waits, **kw):
        self.wait(*waits)
        box.count += 16
        self.work.append(("dma", (out, src, kw), box.sem))
        return box.sem, box.count

    def run(self, eng):
        for kind, what, arg in self.work:
            if kind == "wait":
                eng.wait_ge(what, arg)
            elif kind == "do":
                what(eng).then_inc(self.sem, 1)
            else:
                out, src, kw = what
                eng.dma_start(out, src, **kw).then_inc(arg, 16)


class Box:

    def __init__(self, sem):
        self.sem, self.count = sem, 0


def macaron(nc, a, consts, out, x1_d, z_d, kqv_d, beta_d):
    T = a["L0_attn_x"].shape[1]
    NT, NS = T // TOK, T // SUP
    x_v = a["L0_attn_x"].rearrange("a (t b p) d -> (a t) p b d", b=NB, p=P)
    out_v = out.rearrange("a (t b p) d -> (a t) p b d", b=NB, p=P)
    x1_v = x1_d.rearrange("(t b p) d -> t p b d", b=NB, p=P)
    z_v = z_d.rearrange("(t b p) d -> t p b d", b=NB, p=P)

    top = ExitStack()
    with top:
        def sem(name):
            return top.enter_context(nc.semaphore(name))

        def box(name):
            return Box(sem(name))

        pe, act, dve, pool, sp = (Lane(sem(f"s_{n}")) for n in ("pe", "act", "dve", "pool", "sp"))
        lanes = (pe, act, dve, pool, sp)

        def sbuf(stack, name, shape, dt=F32):
            return stack.enter_context(nc.sbuf_tensor(name, shape, dt))

        bank = [top.enter_context(nc.psum_tensor(f"bank{i}", [P, 512], F32)) for i in range(8)]
        bank_read = [None] * 8

        cst = sbuf(top, "cst", [P, C_END])
        win = sbuf(top, "win", [P, NF, P])
        wout = sbuf(top, "wout", [P, D])
        w1t = sbuf(top, "w1t", [P, 8])
        b1t = sbuf(top, "b1t", [P, 8])
        w2t = sbuf(top, "w2t", [P, 8])
        bint = sbuf(top, "bint", [P, 1])
        b2t = sbuf(top, "b2t", [P, 1])
        boutb = sbuf(top, "boutb", [P, D])
        ident = cst[:, C_ID:C_GM]
        bdmask = cst[:, C_BD:C_EYE]
        eye = cst[:, C_EYE:C_POW]
        neg_half, pos_half = cst[:, C_POW:C_POW + 4], cst[:, C_POW + 8:C_POW + 9]

        d_par = box("d_par")
        W1, B1, W2 = a["L0_ffn_W1"], a["L0_ffn_b1"], a["L0_ffn_W2"]
        col = lambda v: v.rearrange("(p o) -> p o", o=1)
        row = lambda v, n: v.rearrange("(o n) -> o n", o=1).broadcast_to([P, n])
        zb2 = pool.do(lambda e: e.memset(b2t[:, :], 0.0))
        loads = [(cst[:, :], consts), (boutb[:, :], row(a["L0_ffn_bout"], D))]
        for h in range(2):
            r = slice(64 * h, 64 * h + 64)
            loads += [(win[:, :, r], a["L0_ffn_Win"].rearrange("(k p) m -> p k m", p=P)),
                      (wout[r, :], a["L0_ffn_Wout"]),
                      (w1t[r, :], W1[:, 8 * h:8 * h + 8]), (b1t[r, :], B1[:, 8 * h:8 * h + 8]),
                      (w2t[r, :], W2[:, 8 * h:8 * h + 8]), (bint[r, :], col(a["L0_ffn_bin_"]))]
        loads.append((b2t[0:64, :], col(a["L0_ffn_b2"])))
        for o, s in loads:
            par = sp.dma(d_par, o, s, zb2)
        half_w = act.do(lambda e: e.activation(wout[:, :], wout[:, :], ACT.Copy, scale=0.5), par)
        half_b = act.do(lambda e: e.activation(boutb[:, :], boutb[:, :], ACT.Copy, scale=0.5), par)
        fold = dve.do(lambda e: e.scalar_tensor_tensor(b1t[:, :], w1t[:, :], bint[:, 0:1], b1t[:, :],
                                                       ALU.mult, ALU.add), par)
        ready = [par, half_w, half_b, fold]

        def layernorm(buf, stats, mv, rs, nm, got, freed):
            def bn(e):
                for b in range(NB):
                    r = e.bn_stats(stats[:, b, :], buf[:, b, :])
                return r

            def ag(e):
                for b in range(NB):
                    r = e.bn_aggr(mv[:, b, :], stats[:, b, :])
                return r
            t = dve.do(bn, got)
            t = dve.do(ag, t, freed)
            t = pool.do(lambda e: e.tensor_scalar(rs[:, :], mv[:, :, 1], LN_EPS, None, ALU.add), t, freed)
            t_rs = pool.do(lambda e: e.tensor_tensor(rs[:, :], rs[:, :], neg_half, ALU.pow), t)
            t_nm = dve.do(lambda e: e.scalar_tensor_tensor(nm[:, :], mv[:, :, 0], -1.0, rs[:, :],
                                                           ALU.mult, ALU.mult), t_rs)
            return t_nm

        def apply_norm(dst, src, rs, nm, got, freed):
            return [act.do(lambda e, b=b: e.activation(dst[:, b, :], src[:, b, :], ACT.Identity,
                                                       bias=nm[:, b:b + 1], scale=rs[:, b:b + 1]),
                           got, freed) for b in range(NB)]

        def turn(src, f, bk, got):
            def go(e):
                for b in range(NB):
                    r = e.transpose(bank[bk][:, b * P:(b + 1) * P], src[:, b, f * P:(f + 1) * P], ident)
                return r
            return pe.do(go, got, par, bank_read[bk])

        def hidden(xT, got, bk, relu, g, g_free):
            def mm(e):
                for f in range(NF):
                    r = e.matmul(bank[bk][:, :], win[:, f, :], xT[:, f, :], start=f == 0, stop=f == NF - 1)
                return r
            s = pe.do(mm, got, ready, bank_read[bk])
            acc = g_free
            for h in range(8):
                rb = relu[h % 2]
                t = act.do(lambda e, h=h, rb=rb: e.activation(rb["t"][:, :], bank[bk][:, :], ACT.Relu,
                                                              bias=b1t[:, h:h + 1], scale=w1t[:, h:h + 1]),
                           s, rb["read"], ready)
                if h == 0:
                    acc = dve.do(lambda e, rb=rb: e.tensor_scalar(g[:, :], rb["t"][:, :], w2t[:, 0:1],
                                                                  b2t[:, 0:1], ALU.mult, ALU.add), t, acc)
                else:
                    acc = dve.do(lambda e, h=h, rb=rb: e.scalar_tensor_tensor(
                        g[:, :], rb["t"][:, :], w2t[:, h:h + 1], g[:, :], ALU.mult, ALU.add), t, acc)
                rb["read"] = acc
            bank_read[bk] = t
            return s, acc

        def ffn_out(g, got, buf, base, banks):
            done = []
            for b in range(NB):
                bk = banks[b % len(banks)]
                m = pe.do(lambda e, b=b, bk=bk: e.matmul(bank[bk][:, :], g[:, b * P:(b + 1) * P], wout[:, :],
                                                         start=True, stop=True), got, bank_read[bk])
                t = dve.do(lambda e, b=b, bk=bk: e.tensor_tensor(buf[:, b, :], bank[bk][:, :], buf[:, b, :],
                                                                 ALU.add), m, base)
                bank_read[bk] = t
                done.append(t)
            return done, m

        def add_row(buf, rowt, got):
            return [pool.do(lambda e, b=b: e.tensor_tensor(buf[:, b, :], buf[:, b, :], rowt[:, :], ALU.add),
                            got) for b in range(NB)]

        def load_split(pieces, stage, d_stage):
            last = []
            free = [None, None]
            for i, (src, hi, lo) in enumerate(pieces):
                s = stage[i % 2]
                n = hi.shape[-1]
                t = sp.dma(d_stage[i % 2], s[:, 0:n], src, free[i % 2])
                th = act.do(lambda e, s=s, hi=hi, n=n: e.activation(hi, s[:, 0:n], ACT.Copy), t)
                tl = dve.do(lambda e, s=s, hi=hi, lo=lo, n=n: e.tensor_tensor(lo, s[:, 0:n], hi, ALU.subtract),
                            th)
                free[i % 2] = tl
                last = [th, tl]
            return last

        def product(e, o, lhs, rhs, first, last):
            e.matmul(o, lhs[0], rhs[0], start=first, stop=False)
            e.matmul(o, lhs[0], rhs[1], start=False, stop=False)
            return e.matmul(o, lhs[1], rhs[0], start=False, stop=last)

        def barrier():
            now = [(ln.sem, ln.count) for ln in (pe, act, dve, pool) if ln.count]
            for ln in lanes:
                ln.wait(now)

        kinds = ("k", "q", "v")

        def project():
            with ExitStack() as st:
                wp = {}
                stage = [sbuf(st, f"stage{i}", [P, D]) for i in range(2)]
                d_stage = [box(f"d_stage{i}") for i in range(2)]
                pieces = []
                for n in kinds:
                    w = sbuf(st, f"w{n}_hi", [P, NF, D], F32R), sbuf(st, f"w{n}_lo", [P, NF, D], F32R)
                    wp[n] = w
                    pieces += [(a[f"L0_attn_w{n}"][k * P:(k + 1) * P, :], w[0][:, k, :], w[1][:, k, :])
                               for k in range(NF)]
                wbeta = sbuf(st, "wbeta", [P, NF, P])
                wb = sbuf(st, "wb_hi", [P, NF, P], F32R), sbuf(st, "wb_lo", [P, NF, P], F32R)
                bias = {n: sbuf(st, f"b{n}", [P, GROUPS]) for n in kinds}
                bbeta = sbuf(st, "bbeta", [P, 1])
                ln1 = sbuf(st, "ln1", [P, NF])
                d_w = box("d_w")
                z1 = pool.do(lambda e: e.memset(wbeta[:, :, :], 0.0))
                z2 = pool.do(lambda e: e.memset(bbeta[:, :], 0.0))
                wbraw = sbuf(st, "wbraw", [P, NF, HEADS])
                tw = sp.dma(d_w, wbraw[:, :, :], a["L0_attn_wbeta"].rearrange("(k p) h -> p k h", p=P), z2)
                for h in range(4):
                    tw = sp.dma(d_w, bbeta[32 * h:32 * h + GROUPS, :],
                                a["L0_attn_bbeta"].rearrange("(g h o) -> h g o", h=4, o=1)[h], **SHORT)
                for n in kinds:
                    tw = sp.dma(d_w, bias[n][:, :], a[f"L0_attn_b{n}"].rearrange("(g p) -> p g", p=P), **SHORT)
                tw = sp.dma(d_w, ln1[:, :], a["L0_attn_ln1_scale"].rearrange("(g p) -> p g", p=P), **SHORT)
                for h in range(4):
                    z1 = dve.do(lambda e, h=h: e.tensor_copy(wbeta[:, :, 32 * h:32 * h + GROUPS],
                                                             wbraw[:, :, h:HEADS:4]), tw, z1)
                t = act.do(lambda e: e.activation(wb[0][:, :, :], wbeta[:, :, :], ACT.Copy), z1)
                t2 = dve.do(lambda e: e.tensor_tensor(wb[1][:, :, :], wbeta[:, :, :], wb[0][:, :, :], ALU.subtract), t)
                w_ready = load_split(pieces, stage, d_stage) + [t, t2, tw]

                X = [sbuf(st, f"X{i}", [P, NB, D]) for i in range(2)]
                Y = [sbuf(st, f"Y{i}", [P, NB, D]) for i in range(2)]
                xT = sbuf(st, "xT", [P, NF, TOK])
                hT = [(sbuf(st, f"hT{i}_hi", [P, NF, TOK], F32R), sbuf(st, f"hT{i}_lo", [P, NF, TOK], F32R))
                      for i in range(2)]
                relu = [dict(t=sbuf(st, f"relu{i}", [P, TOK]), read=None) for i in range(2)]
                g = [sbuf(st, f"g{i}", [P, TOK]) for i in range(2)]
                stats = sbuf(st, "stats", [P, NB, 6])
                mv = [sbuf(st, f"mv{i}", [P, NB, 2]) for i in range(2)]
                rs = [sbuf(st, f"rs{i}", [P, NB]) for i in range(2)]
                nm = [sbuf(st, f"nm{i}", [P, NB]) for i in range(2)]
                ri = sbuf(st, "ri", [P, NB])
                proj = [sbuf(st, f"proj{i}", [P, TOK]) for i in range(4)]
                d_x = [box(f"d_x{i}") for i in range(2)]
                d_x1 = [box(f"d_x1{i}") for i in range(2)]
                d_proj = [box(f"d_proj{i}") for i in range(4)]
                T1 = {}
                x1_stored = [None, None]
                proj_stored = [None] * 4

                def s1(t):
                    i = t % 2
                    got = sp.dma(d_x[i], X[i][:, :, :], x_v[t], x1_stored[i])
                    tn = layernorm(X[i], stats, mv[0], rs[0], nm[0], got, T1.get(("xn", t - 1)))
                    xn = apply_norm(Y[i], X[i], rs[0], nm[0], tn, T1.get(("hturn", t - 2)))
                    T1["xn", t] = xn
                    T1["xb", t] = add_row(X[i], boutb, [xn, half_b])
                    free = T1.get(("win", t - 1))
                    ends = []
                    for f in range(NF):
                        bk = 3 + f % 2
                        m = turn(Y[i], f, bk, xn)
                        e_ = act.do(lambda e, f=f, bk=bk: e.activation(xT[:, f, :], bank[bk][:, :], ACT.Copy), m, free)
                        bank_read[bk] = e_
                        ends.append(e_)
                    T1["xT", t], T1["xturn", t] = ends, m

                def s2(t):
                    i = t % 2
                    s, acc = hidden(xT, T1["xT", t], 5, relu, g[i], T1.get(("wout", t - 2)))
                    T1["win", t], T1["g", t] = s, acc

                def s3(t):
                    i = t % 2
                    x1, m = ffn_out(g[i], T1["g", t], X[i], T1["xb", t], (6, 7))
                    T1["wout", t] = m
                    tn = layernorm(X[i], stats, mv[1], rs[1], nm[1], x1, T1.get(("h", t - 1)))
                    q = dve.do(lambda e: e.tensor_tensor(ri[:, :], rs[1][:, :], rs[1][:, :], ALU.mult), tn,
                               T1.get(("h", t - 1)))
                    q = dve.do(lambda e: e.tensor_tensor(ri[:, :], ri[:, :], mv[1][:, :, 1], ALU.mult), q)
                    q = dve.do(lambda e: e.tensor_scalar(ri[:, :], ri[:, :], RMS_EPS, None, ALU.add), q)
                    q = pool.do(lambda e: e.tensor_tensor(ri[:, :], ri[:, :], neg_half, ALU.pow), q)
                    y = apply_norm(Y[i], X[i], rs[1], nm[1], tn, T1["xturn", t])
                    h = []
                    for b in range(NB):
                        h.append(dve.do(lambda e, b=b: e.tensor_scalar(Y[i][:, b, :], Y[i][:, b, :], ri[:, b:b + 1],
                                                                       None, ALU.mult), y, q))
                    T1["h", t] = h
                    x1_stored[i] = sp.dma(d_x1[i], x1_v[t], X[i][:, :, :], x1)
                    T1["x1read", t] = y
                    x1_stored[i] = [x1_stored[i], y]

                def s4(t):
                    i = t % 2
                    hi, lo = hT[i]
                    free = T1.get(("proj", t - 2))
                    ends = []
                    for f in range(NF):
                        bk = 3 + f % 2
                        m = turn(Y[i], f, bk, T1["h", t])
                        th = act.do(lambda e, f=f, bk=bk: e.activation(hi[:, f, :], bank[bk][:, :], ACT.Copy,
                                                                       scale=ln1[:, f:f + 1]), m, free, tw)
                        tl = dve.do(lambda e, f=f, bk=bk: e.scalar_tensor_tensor(
                            lo[:, f, :], bank[bk][:, :], ln1[:, f:f + 1], hi[:, f, :], ALU.mult, ALU.subtract),
                            m, th, free)
                        bank_read[bk] = tl
                        ends.append(tl)
                    T1["hT", t], T1["hturn", t] = ends, m

                def s5(t, part):
                    i = t % 2
                    for n in range(13)[part * 5:part * 5 + 5]:
                        bk, slot = n % 3, n % 4

                        def mm(e, n=n, bk=bk):
                            for f in range(NF):
                                w = wb if n == 12 else wp[kinds[n // 4]]
                                c = slice(0, P) if n == 12 else slice((n % 4) * P, (n % 4 + 1) * P)
                                r = product(e, bank[bk][:, :], (w[0][:, f, c], w[1][:, f, c]),
                                            (hT[i][0][:, f, :], hT[i][1][:, f, :]), f == 0, f == NF - 1)
                            return r
                        m = pe.do(mm, T1["hT", t], w_ready, bank_read[bk])
                        if n == 12:
                            dst = beta_d[:, t * TOK:(t + 1) * TOK]
                            ev = act.do(lambda e, bk=bk, slot=slot: e.activation(
                                proj[slot][:, :], bank[bk][:, :], ACT.Sigmoid, bias=bbeta[:, 0:1]),
                                m, proj_stored[slot])
                        else:
                            dst = kqv_d[n // 4, n % 4, :, t * TOK:(t + 1) * TOK]
                            ev = act.do(lambda e, n=n, bk=bk, slot=slot: e.activation(
                                proj[slot][:, :], bank[bk][:, :], ACT.Identity,
                                bias=bias[kinds[n // 4]][:, n % 4:n % 4 + 1]), m, proj_stored[slot])
                        bank_read[bk] = ev
                        proj_stored[slot] = sp.dma(d_proj[slot], dst, proj[slot][:, :], ev)
                    T1["proj", t] = m

                s1(0)
                s2(0)
                s3(0)
                s1(1)
                s4(0)
                for t in range(NT):
                    s5(t, 0)
                    if t + 1 < NT:
                        s2(t + 1)
                    s5(t, 1)
                    if t + 1 < NT:
                        s3(t + 1)
                    s5(t, 2)
                    if t + 2 < NT:
                        s1(t + 2)
                    if t + 1 < NT:
                        s4(t + 1)
                return [proj_stored, x1_stored]

        stored1 = project()
        barrier()
        for ln in lanes:
            ln.wait(stored1)

        def delta():
            with ExitStack() as st:
                wo = sbuf(st, "wo", [P, NF, D])
                bo = sbuf(st, "bo", [P, D])
                kq = sbuf(st, "kq", [P, 2, NU, CH])
                vk = sbuf(st, "vk", [P, 2, NU, HD])
                pk = sbuf(st, "pk", [P, 2, NU, HD])
                lt = sbuf(st, "lt", [P, NU, CH])
                raw = sbuf(st, "raw", [P, NU, CH])
                sysb = raw[:, :, :].rearrange("p (i h) j -> p i h j", h=4)
                tmp = sbuf(st, "tmp", [P, 4 * 16 * 16])
                bT = tmp[:, 0:SUP]
                bs = sbuf(st, "bs", [P, NC, CH])
                nrm = sbuf(st, "nrm", [P, NU])
                rn = sbuf(st, "rn", [P, NU])
                bdk = [sbuf(st, f"bdk{i}", [P, 4, 4, CH]) for i in range(2)]
                bdur = [sbuf(st, f"bdur{i}", [P, 4, 2, 4, CH]) for i in range(2)]
                bdf = [sbuf(st, f"bdf{i}", [P, 4, 4, CH]) for i in range(2)]
                bds = [sbuf(st, f"bds{i}", [P, 4, 4, CH]) for i in range(2)]
                ur = [sbuf(st, f"ur{i}", [P, 4, 2, HD]) for i in range(2)]
                op = [sbuf(st, f"op{i}", [P, 4, 2, HD]) for i in range(2)]
                gt = [sbuf(st, f"gt{i}", [P, 4, CH]) for i in range(2)]
                psi = [sbuf(st, f"psi{i}", [P, 4, HD]) for i in range(2)]
                fi = [sbuf(st, f"fi{i}", [P, 4, HD]) for i in range(2)]
                sT = [sbuf(st, f"sT{i}", [P, 4, HD]) for i in range(2)]
                oT = [sbuf(st, f"oT{i}", [P, GROUPS, P]) for i in range(2)]
                x1b = [sbuf(st, f"x1b{i}", [P, D]) for i in range(2)]
                zb = [sbuf(st, f"zb{i}", [P, D]) for i in range(2)]
                stat2 = [sbuf(st, f"stat2{i}", [P, 6]) for i in range(2)]
                mv2 = [sbuf(st, f"mv2{i}", [P, 2]) for i in range(2)]
                rs2 = [sbuf(st, f"rs2{i}", [P, 1]) for i in range(2)]
                nm2 = [sbuf(st, f"nm2{i}", [P, 1]) for i in range(2)]
                d_wo, d_q, d_k, d_v, d_b = box("d_wo"), box("d_q"), box("d_k"), box("d_v"), box("d_b")
                d_x1b = [box(f"d_x1b{i}") for i in range(2)]
                d_z = [box(f"d_z{i}") for i in range(2)]
                two = sp.dma(d_wo, wo[:, :, :], a["L0_attn_wo"].rearrange("(k p) n -> p k n", p=P))
                two = sp.dma(d_wo, bo[:, :], row(a["L0_attn_bo"], D))
                gmask = cst[:, C_GM:C_BD].rearrange("p (s i) -> p s i", s=2)
                state = dve.do(lambda e: e.memset(sT[0][:, :, :], 0.0))
                zs = pool.do(lambda e: e.memset(bds[0][:, :, :, :], 0.0))
                E = {}

                def bd_build(lane, dst, src, n, *waits):
                    return lane.do(lambda e: e.tensor_tensor(
                        dst, src.unsqueeze(2).broadcast_to([P, n, 4, CH]),
                        bdmask.unsqueeze(1).unsqueeze(3).broadcast_to([P, n, 4, CH]), ALU.mult), *waits)

                for s in range(NS):
                    cols = slice(s * SUP, (s + 1) * SUP)
                    done = E.get("super")
                    src = [kqv_d[n, :, :, cols].rearrange("g p (c j) -> p g c j", j=CH) for n in range(3)]
                    view = lambda b: b.rearrange("p (g c) j -> p g c j", g=GROUPS)
                    tb = sp.dma(d_b, bT, beta_d[:, cols], done)
                    tk = sp.dma(d_k, view(raw[:, :, :]), src[0], done)
                    tq = sp.dma(d_q, view(kq[:, 1, :, :]), src[1], done)
                    tb = dve.do(lambda e: e.transpose(bs[:, :, :].rearrange("p c g -> p (c g)"), bT), tb, done)
                    K = vk[:, 1, :, :]
                    flat = lambda v: v.rearrange("p u j -> p (u j)")
                    t = dve.do(lambda e: e.transpose(flat(K), flat(raw[:, :, :])), tk, done)
                    sq = act.do(lambda e: e.activation(raw[:, :, :], K, ACT.Square), t)
                    t = dve.do(lambda e: e.tensor_reduce(nrm[:, :], raw[:, :, :], AX.X, ALU.add), sq)
                    t_red = t
                    t = pool.do(lambda e: e.tensor_tensor(nrm[:, :], nrm[:, :], pos_half.broadcast_to([P, NU]),
                                                          ALU.pow), t)
                    t = dve.do(lambda e: e.tensor_scalar(nrm[:, :], nrm[:, :], NORM_EPS, None, ALU.add), t)
                    t = dve.do(lambda e: e.reciprocal(rn[:, :], nrm[:, :]), t)
                    kn = dve.do(lambda e: e.tensor_tensor(K, K, rn[:, :].unsqueeze(2).broadcast_to([P, NU, HD]),
                                                          ALU.mult), t)
                    tv = sp.dma(d_v, view(raw[:, :, :]), src[2], t_red)
                    kb = pool.do(lambda e: e.tensor_tensor(
                        pk[:, 1, :, :].rearrange("p (g c) j -> p g c j", g=GROUPS),
                        K.rearrange("p (g c) j -> p g c j", g=GROUPS),
                        bs[:, :, 0:GROUPS].rearrange("p c g -> p g c").unsqueeze(3)
                        .broadcast_to([P, GROUPS, NC, HD]), ALU.mult), kn, tb, done)
                    kT = dve.do(lambda e: e.transpose(flat(kq[:, 0, :, :]), flat(K)), kn, done)
                    vT = dve.do(lambda e: e.transpose(flat(vk[:, 0, :, :]), flat(raw[:, :, :])), tv, done)
                    kbT = dve.do(lambda e: e.transpose(flat(raw[:, :, :]), flat(pk[:, 1, :, :])), kb, vT)
                    for u8 in range(0, NU, 8):
                        bk = (u8 // 8) % 2
                        halves = []
                        for q in range(2):
                            k = (u8 // 4 + q) % 2
                            u = u8 + 4 * q
                            tbd = bd_build(pool, bdk[k][:, :, :, :], raw[:, u:u + 4, :], 4, kbT, E.get(("bdk", k)))

                            def gram(e, k=k, u=u, q=q, bk=bk):
                                for n in range(4):
                                    o = bank[bk][:, (4 * q + n) * 64:(4 * q + n + 1) * 64]
                                    r = e.matmul(o.rearrange("p (s i) -> p s i", s=2),
                                                 bdk[k][:, n, :, :].rearrange("p h j -> p (h j)"),
                                                 kq[:, :, u + n, :], start=True, stop=True)
                                return r
                            m = pe.do(gram, tbd, kT, tq, bank_read[bk])
                            E["bdk", k] = m
                        gb = bank[bk][:, :].rearrange("p (u s i) -> p u s i", s=2, i=CH)
                        t1 = dve.do(lambda e, gb=gb, u8=u8: e.tensor_tensor(
                            lt[:, u8:u8 + 8, :], gb[:, :, 0, :],
                            gmask[:, 0:1, :].broadcast_to([P, 8, CH]), ALU.mult), m, done)
                        t2 = dve.do(lambda e, gb=gb, u8=u8: e.tensor_tensor(
                            pk[:, 0, u8:u8 + 8, :], gb[:, :, 1, :],
                            gmask[:, 1:2, :].broadcast_to([P, 8, CH]), ALU.mult), m, done)
                        bank_read[bk] = t2
                    tin = []
                    for i4 in range(0, CH, 4):
                        bk = 2 + (i4 // 4) % 2

                        def go(e, i4=i4, bk=bk):
                            for n in range(4):
                                r = e.transpose(bank[bk][:, n * P:(n + 1) * P], lt[:, :, i4 + n], ident)
                            return r
                        m = pe.do(go, t1, bank_read[bk])
                        ev = act.do(lambda e, i4=i4, bk=bk: e.activation(
                            sysb[:, i4:i4 + 4, :, :].rearrange("p i h j -> p (i h j)"), bank[bk][:, :], ACT.Copy),
                            m, done)
                        bank_read[bk] = ev
                    t = ev
                    N = sysb.rearrange("p i h j -> p h i j")
                    for j in range(1, CH - 1):
                        rows = CH - 1 - j
                        tt = tmp[:, 0:4 * rows * j].rearrange("p (h i k) -> p h i k", h=4, i=rows)
                        t = dve.do(lambda e, j=j, rows=rows, tt=tt: e.tensor_tensor(
                            tt, N[:, :, j + 1:CH, j:j + 1].broadcast_to([P, 4, rows, j]),
                            N[:, :, j:j + 1, 0:j].broadcast_to([P, 4, rows, j]), ALU.mult), t)
                        t = dve.do(lambda e, j=j, tt=tt: e.tensor_tensor(
                            N[:, :, j + 1:CH, 0:j], N[:, :, j + 1:CH, 0:j], tt, ALU.add), t)
                    solved = t
                    for i4 in range(0, CH, 4):
                        bk = 2 + (i4 // 4) % 2

                        def back(e, i4=i4, bk=bk):
                            for n in range(4):
                                r = e.transpose(bank[bk][:, n * P:(n + 1) * P],
                                                sysb[:, i4 + n, :, :].rearrange("p h j -> p (h j)"), ident)
                            return r
                        m = pe.do(back, solved, bank_read[bk])
                        ev = act.do(lambda e, i4=i4, bk=bk: e.activation(
                            lt[:, :, i4:i4 + 4].rearrange("p u i -> p i u"),
                            bank[bk][:, :].rearrange("p (i u) -> p i u", i=4), ACT.Copy), m)
                        bank_read[bk] = ev
                    nt = ev
                    unit = lambda b, c: b.rearrange("p (g c) j -> p g c j", g=GROUPS)[:, :, c, :]
                    for c in range(NC):
                        k = c % 2
                        o2 = (c // 4) % 2
                        bn_ = bd_build(pool, bdk[k][:, :, :, :], unit(lt[:, :, :], c), 4, nt, E.get(("bdk", k)))

                        def mm_ur(e, c=c, k=k):
                            for n in range(4):
                                r = e.matmul(bank[4][:, n * 64:(n + 1) * 64].rearrange("p (s j) -> p s j", s=2),
                                             bdk[k][:, n, :, :].rearrange("p h j -> p (h j)"),
                                             vk[:, :, n * NC + c, :], start=True, stop=True)
                            return r
                        m = pe.do(mm_ur, bn_, bank_read[4], vT, kn)
                        E["bdk", k] = m
                        ps = bank[4][:, 0:256].rearrange("p (g s j) -> p g s j", g=4, s=2)
                        for s_ in range(2):
                            t = dve.do(lambda e, s_=s_, c=c, k=k, ps=ps: e.tensor_tensor(
                                ur[k][:, :, s_, :], ps[:, :, s_, :], unit(vk[:, s_, :, :], c), ALU.add),
                                m, E.get(("bdur", k)))
                            E["ur", s_] = t
                        bank_read[4] = t
                        t = dve.do(lambda e, k=k: e.tensor_tensor(
                            bdur[k][:, :, :, :, :].rearrange("p g s h j -> p (g s) h j"),
                            ur[k][:, :, :, :].rearrange("p g s j -> p (g s) j").unsqueeze(2)
                            .broadcast_to([P, 8, 4, CH]),
                            bdmask.unsqueeze(1).unsqueeze(3).broadcast_to([P, 8, 4, CH]), ALU.mult),
                            t, E["ur", 0], E.get(("ok", k)))
                        E["bdur", k] = t

                        def mm_out(e, c=c, k=k):
                            for sd in range(2):
                                for n in range(4):
                                    o = bank[5][:, (4 * sd + n) * 64:(4 * sd + n + 1) * 64]
                                    r = e.matmul(o.rearrange("p (s j) -> p s j", s=2),
                                                 bdur[k][:, n, sd, :, :].rearrange("p h j -> p (h j)"),
                                                 pk[:, :, n * NC + c, :], start=True, stop=True)
                            return r
                        m = pe.do(mm_out, t, t2, kb, bank_read[5])
                        E["ok", k] = m
                        ps = bank[5][:, :].rearrange("p (d g s j) -> p d g s j", d=2, g=4, s=2)
                        to = act.do(lambda e, k=k, ps=ps: e.activation(op[k][:, :, :, :], ps[:, 0, :, :, :], ACT.Copy),
                                    m, E.get(("o", k)), E.get(("psi", k)))
                        tg = dve.do(lambda e, c=c, k=k, ps=ps: e.tensor_tensor(
                            gt[k][:, :, :], unit(kq[:, 1, :, :], c), ps[:, 1, :, 0, :], ALU.subtract),
                            m, to, tq, E.get(("sg", k)))
                        tf = dve.do(lambda e, k=k, ps=ps: e.tensor_tensor(
                            fi[k][:, :, :], eye.unsqueeze(1).broadcast_to([P, 4, HD]), ps[:, 1, :, 1, :],
                            ALU.subtract), m, to, E.get(("bdf", k)))
                        bank_read[5] = tf
                        tf = bd_build(dve, bdf[k][:, :, :, :], fi[k][:, :, :], 4, tf, E.get(("step", k)))
                        E["bdf", k] = tf
                        tp = dve.do(lambda e, k=k: e.transpose(psi[k][:, :, :],
                                                               op[k][:, :, 1, :]), to, E.get(("st", k)))
                        E["psi", k] = tp

                        def mm_s(e, k=k):
                            for n in range(4):
                                r = e.matmul(bank[6][:, n * 32:(n + 1) * 32],
                                             bdf[k][:, n, :, :].rearrange("p h j -> p (h j)"),
                                             sT[k][:, n, :], start=True, stop=True)
                            return r
                        m_s = pe.do(mm_s, tf, state, bank_read[6])
                        E["step", k] = m_s

                        def mm_g(e, k=k):
                            for n in range(4):
                                r = e.matmul(bank[7][:, n * 32:(n + 1) * 32],
                                             bds[k][:, n, :, :].rearrange("p h j -> p (h j)"),
                                             gt[k][:, n, :], start=True, stop=True)
                            return r
                        m_g = pe.do(mm_g, zs, tg, bank_read[7])
                        E["sg", k] = m_g
                        state = dve.do(lambda e, k=k: e.tensor_tensor(
                            sT[1 - k][:, :, :], bank[6][:, 0:P].rearrange("p (g d) -> p g d", g=4),
                            psi[k][:, :, :], ALU.add), m_s, tp, E.get(("step", 1 - k)), E.get(("bdsr", 1 - k)))
                        bank_read[6] = state
                        E["st", k] = state
                        zs = bd_build(pool, bds[1 - k][:, :, :, :], sT[1 - k][:, :, :], 4, state,
                                      E.get(("sg", 1 - k)))
                        E["bdsr", 1 - k] = zs
                        t_o = dve.do(lambda e, c=c, k=k, o2=o2: e.tensor_tensor(
                            oT[o2][:, :, (c % 4) * CH:(c % 4 + 1) * CH],
                            bank[7][:, 0:P].rearrange("p (g d) -> p g d", g=4),
                            op[k][:, :, 0, :], ALU.add), m_g, to, E.get(("wo", o2)) if c % 4 == 0 else None)
                        bank_read[7] = t_o
                        E["o", k] = t_o
                        if c % 4 == 3:
                            blk = s * (SUP // P) + c // 4
                            tx = sp.dma(d_x1b[o2], x1b[o2][:, :], x1_d[blk * P:(blk + 1) * P, :], E.get(("y", o2)))
                            q = dve.do(lambda e, o2=o2: e.bn_stats(stat2[o2][:, :], x1b[o2][:, :]), tx)
                            q = dve.do(lambda e, o2=o2: e.bn_aggr(mv2[o2][:, :], stat2[o2][:, :]), q, E.get(("y", o2)))
                            q = pool.do(lambda e, o2=o2: e.tensor_scalar(rs2[o2][:, :], mv2[o2][:, 1:2], LN_EPS, None,
                                                                         ALU.add), q, E.get(("y", o2)))
                            q = pool.do(lambda e, o2=o2: e.tensor_tensor(rs2[o2][:, :], rs2[o2][:, :],
                                                                         neg_half[:, 0:1], ALU.pow), q)
                            q = dve.do(lambda e, o2=o2: e.scalar_tensor_tensor(
                                nm2[o2][:, :], mv2[o2][:, 0:1], -1.0, rs2[o2][:, :], ALU.mult, ALU.mult), q)
                            y = act.do(lambda e, o2=o2: e.activation(zb[o2][:, :], x1b[o2][:, :], ACT.Identity,
                                                                     bias=nm2[o2][:, 0:1], scale=rs2[o2][:, 0:1]),
                                       q, E.get(("z", o2)))
                            E["y", o2] = y
                            yb = pool.do(lambda e, o2=o2: e.tensor_tensor(zb[o2][:, :], zb[o2][:, :], bo[:, :],
                                                                          ALU.add), y, two)
                            wb_ = o2

                            def mm_wo(e, o2=o2, wb_=wb_):
                                for f in range(NF):
                                    r = e.matmul(bank[wb_][:, :], oT[o2][:, f, :], wo[:, f, :],
                                                 start=f == 0, stop=f == NF - 1)
                                return r
                            m = pe.do(mm_wo, t_o, two, bank_read[wb_])
                            E["wo", o2] = m
                            t = dve.do(lambda e, o2=o2, wb_=wb_: e.tensor_tensor(
                                zb[o2][:, :], bank[wb_][:, :], zb[o2][:, :], ALU.add), m, yb)
                            bank_read[wb_] = t
                            E["z", o2] = sp.dma(d_z[o2], z_d[blk * P:(blk + 1) * P, :], zb[o2][:, :], t)
                    E["super"] = [m_g, t_o, E["ok", 0], E["ok", 1], E["bdk", 0], E["bdk", 1], tg]
                return [E["z", 0], E["z", 1]]

        stored2 = delta()
        barrier()
        for ln in lanes:
            ln.wait(stored2)

        def dense():
            with ExitStack() as st:
                w1 = sbuf(st, "w1_hi", [P, NF, DFF], F32R), sbuf(st, "w1_lo", [P, NF, DFF], F32R)
                w2 = sbuf(st, "w2_hi", [P, NM, D], F32R), sbuf(st, "w2_lo", [P, NM, D], F32R)
                b1m = sbuf(st, "b1m", [P, NM])
                ln2 = sbuf(st, "ln2", [P, NF])
                b2b = sbuf(st, "b2b", [P, D])
                hT = sbuf(st, "h2_hi", [P, NF, TOK], F32R), sbuf(st, "h2_lo", [P, NF, TOK], F32R)
                xT = sbuf(st, "x2T", [P, NF, TOK])
                Z = sbuf(st, "Z", [P, NB, D])
                S = sbuf(st, "S", [P, NB, D])
                H = sbuf(st, "H", [P, NB, D])
                gl = [sbuf(st, f"gl{i}", [P, TOK]) for i in range(2)]
                gh = [(sbuf(st, f"gh{i}", [P, TOK], F32R), sbuf(st, f"glo{i}", [P, TOK], F32R)) for i in range(2)]
                g = sbuf(st, "g3", [P, TOK])
                stats = sbuf(st, "stats3", [P, NB, 6])
                mv = sbuf(st, "mv3", [P, NB, 2])
                rs = sbuf(st, "rs3", [P, NB])
                nm = sbuf(st, "nm3", [P, NB])
                ss = sbuf(st, "ss3", [P, NB])
                relu = [dict(t=sbuf(st, f"relu3{i}", [P, TOK]), read=None) for i in range(1)] * 2
                d_w = box("d_w3")
                d_Z, d_S, d_out = box("d_Z"), box("d_S"), box("d_out")
                tw = sp.dma(d_w, b1m[:, :], a["L0_attn_b1"].rearrange("(g p) -> p g", p=P), **SHORT)
                tw = sp.dma(d_w, ln2[:, :], a["L0_attn_ln2_scale"].rearrange("(g p) -> p g", p=P), **SHORT)
                tw = sp.dma(d_w, b2b[:, :], row(a["L0_attn_b2"], D))
                pieces = []
                for k in range(NF):
                    for n in range(4):
                        c = slice(n * D, (n + 1) * D)
                        pieces.append((a["L0_attn_w1"][k * P:(k + 1) * P, c], w1[0][:, k, c], w1[1][:, k, c]))
                for m in range(NM):
                    pieces.append((a["L0_attn_w2"][m * P:(m + 1) * P, :], w2[0][:, m, :], w2[1][:, m, :]))
                d_st3 = [box("d_st3a"), box("d_st3b")]
                w_ready = load_split(pieces, [xT[:, 0, :], xT[:, 1, :]], d_st3) + [tw]
                R = {}

                def front(t):
                    got = sp.dma(d_Z, Z[:, :, :], z_v[t], R.get("s"), R.get("hs"))

                    def sq(e):
                        for b in range(NB):
                            r = e.activation(H[:, b, :], Z[:, b, :], ACT.Square, accum_out=ss[:, b:b + 1])
                        return r
                    q = act.do(sq, got, R.get("xturn"), R.get("hs"))
                    q = dve.do(lambda e: e.tensor_scalar(ss[:, :], ss[:, :], 1.0 / D, RMS_EPS, ALU.mult, ALU.add), q)
                    q = pool.do(lambda e: e.tensor_tensor(ss[:, :], ss[:, :], neg_half, ALU.pow), q)
                    h = [dve.do(lambda e, b=b: e.tensor_scalar(H[:, b, :], Z[:, b, :], ss[:, b:b + 1], None,
                                                               ALU.mult), q) for b in range(NB)]
                    R["hs"] = h
                    for f in range(NF):
                        bk = 6 + f % 2
                        m = turn(H, f, bk, h)
                        th = act.do(lambda e, f=f, bk=bk: e.activation(hT[0][:, f, :], bank[bk][:, :], ACT.Copy,
                                                                       scale=ln2[:, f:f + 1]), m, R.get("w1"), tw)
                        tl = dve.do(lambda e, f=f, bk=bk: e.scalar_tensor_tensor(
                            hT[1][:, f, :], bank[bk][:, :], ln2[:, f:f + 1], hT[0][:, f, :], ALU.mult, ALU.subtract),
                            th)
                        bank_read[bk] = tl
                    R["hT"], R["hturn"] = tl, m

                def residual(t):
                    got = sp.dma(d_S, S[:, :, :], x1_v[t], R.get("out"))
                    q = [pool.do(lambda e, b=b: e.tensor_tensor(S[:, b, :], S[:, b, :], Z[:, b, :], ALU.add), got)
                         for b in range(NB)]
                    R["s"] = q
                    R["sb"] = add_row(S, b2b, [q, tw])

                def mlp_up(m):
                    bk, k = m % 2, m % 2

                    def mm(e):
                        c = slice(m * P, (m + 1) * P)
                        for f in range(NF):
                            r = product(e, bank[bk][:, :], (w1[0][:, f, c], w1[1][:, f, c]),
                                        (hT[0][:, f, :], hT[1][:, f, :]), f == 0, f == NF - 1)
                        return r
                    t = pe.do(mm, R["hT"], w_ready, bank_read[bk])
                    R["w1"] = t
                    t = act.do(lambda e: e.activation(gl[k][:, :], bank[bk][:, :], ACT.Gelu_apprx_tanh,
                                                      bias=b1m[:, m:m + 1]), t, R.get(("gl", k)))
                    bank_read[bk] = t
                    th = act.do(lambda e: e.activation(gh[k][0][:, :], gl[k][:, :], ACT.Copy), t, R.get(("gh", k)))
                    tl = dve.do(lambda e: e.tensor_tensor(gh[k][1][:, :], gl[k][:, :], gh[k][0][:, :], ALU.subtract),
                                th, R.get(("gh", k)))
                    R["gl", k], R["up", m] = tl, tl

                def mlp_down(m):
                    k = m % 2

                    def mm(e):
                        for b in range(NB):
                            r = product(e, bank[2 + b][:, :], [x[:, b * P:(b + 1) * P] for x in gh[k]],
                                        (w2[0][:, m, :], w2[1][:, m, :]), m == 0, m == NM - 1)
                        return r
                    t = pe.do(mm, R["up", m], bank_read[2:6] if m == 0 else None)
                    R["gh", k], R["down"] = t, t

                def x2(t):
                    ends = []
                    for b in range(NB):
                        q = dve.do(lambda e, b=b: e.tensor_tensor(S[:, b, :], bank[2 + b][:, :], S[:, b, :], ALU.add),
                                   R["down"], R["sb"])
                        bank_read[2 + b] = q
                        ends.append(q)
                    R["x2"] = ends

                def ffn_front(t):
                    tn = layernorm(S, stats, mv, rs, nm, R["x2"], R.get("xn"))
                    xn = apply_norm(H, S, rs, nm, tn, [R["hturn"], R.get("xturn")])
                    R["xn"] = xn
                    R["xb"] = add_row(S, boutb, xn)
                    for f in range(NF):
                        bk = 6 + f % 2
                        m = turn(H, f, bk, xn)
                        e_ = act.do(lambda e, f=f, bk=bk: e.activation(xT[:, f, :], bank[bk][:, :], ACT.Copy), m,
                                    R.get("win"), w_ready)
                        bank_read[bk] = e_
                    R["xT"], R["xturn"] = e_, m

                def ffn_mid(t):
                    R["win"], R["g"] = hidden(xT, R["xT"], 6, relu, g, R.get("wout"))

                def ffn_end(t):
                    x3, R["wout"] = ffn_out(g, R["g"], S, R["xb"], (7,))
                    R["out"] = sp.dma(d_out, out_v[t], S[:, :, :], x3)

                front(0)
                for t in range(NT):
                    for m in range(NM):
                        mlp_up(m)
                        if m:
                            mlp_down(m - 1)
                        if t and m == 1:
                            ffn_front(t - 1)
                        if t and m == 4:
                            ffn_mid(t - 1)
                        if t and m == 9:
                            ffn_end(t - 1)
                        if m == 11:
                            residual(t)
                    if t + 1 < NT:
                        front(t + 1)
                    mlp_down(NM - 1)
                    x2(t)
                ffn_front(NT - 1)
                ffn_mid(NT - 1)
                ffn_end(NT - 1)
                return R["out"]

        stored3 = dense()
        sp.wait(stored1, stored2, stored3)

        block = top.enter_context(nc.Block())

        @block.sync
        def _(eng):
            sp.run(eng)

        @block.scalar
        def _(eng):
            act.run(eng)

        @block.vector
        def _(eng):
            dve.run(eng)

        @block.gpsimd
        def _(eng):
            pool.run(eng)

        @block.tensor
        def _(eng):
            pe.run(eng)


_INS = ['L0_attn_x', 'L0_attn_wq', 'L0_attn_bq', 'L0_attn_wk', 'L0_attn_bk', 'L0_attn_wv', 'L0_attn_bv',
        'L0_attn_wbeta', 'L0_attn_bbeta', 'L0_attn_wo', 'L0_attn_bo', 'L0_attn_w1', 'L0_attn_b1', 'L0_attn_w2',
        'L0_attn_b2', 'L0_attn_ln1_scale', 'L0_attn_ln2_scale', 'L0_ffn_Win', 'L0_ffn_bin_', 'L0_ffn_W1',
        'L0_ffn_b1', 'L0_ffn_W2', 'L0_ffn_b2', 'L0_ffn_Wout', 'L0_ffn_bout']


def kernel(**inputs):
    import numpy as _np
    import concourse.bacc as _bacc
    from concourse import mybir as _mybir
    from concourse.bass_utils import run_bass_kernel_spmd as _run

    nc = _bacc.Bacc("TRN2", target_bir_lowering=False, num_devices=1)
    f32 = _mybir.dt.float32
    arrays, args = {}, {}
    for name in _INS:
        v = _np.ascontiguousarray(inputs[name])
        arrays[f"in_{name}"] = v
        args[name] = nc.dram_tensor(f"in_{name}", v.shape, _mybir.dt.from_np(v.dtype), kind="ExternalInput").ap()
    arrays["consts"] = shape_constants()
    consts = nc.dram_tensor("consts", arrays["consts"].shape, f32, kind="ExternalInput").ap()
    shape = inputs['L0_attn_x'].shape
    T = shape[1]
    out = nc.dram_tensor("out", shape, f32, kind="ExternalOutput").ap()
    x1_d = nc.dram_tensor("x1_scratch", (T, D), f32).ap()
    z_d = nc.dram_tensor("z_scratch", (T, D), f32).ap()
    kqv_d = nc.dram_tensor("kqv_scratch", (3, GROUPS, P, T), f32).ap()
    beta_d = nc.dram_tensor("beta_scratch", (P, T), f32).ap()
    macaron(nc, args, consts, out, x1_d, z_d, kqv_d, beta_d)
    r = _run(nc, [arrays], core_ids=[0])
    return r.results[0]["out"]
```

```python
from contextlib import ExitStack

import concourse.bass as bass
import concourse.mybir as mybir
import numpy as np

F32 = mybir.dt.float32
F32R = mybir.dt.float32r
ALU = mybir.AluOpType
ACT = mybir.ActivationFunctionType
AX = mybir.AxisListType

P = 128
D = 512
NF = D // P
HEADS, HD = 16, 32
GROUPS = HEADS // 4
DFF = 2048
NM = DFF // P
TOK = 512
NB = TOK // P
SUP = 1024
CH = 32
NC = SUP // CH
NU = GROUPS * NC
TC = TOK // CH
TU = GROUPS * TC
P1, V1, K1, Q1, KT1 = range(5)
B2, P2, V2, K2, Q2 = range(5)
WIDE = 3 * CH
LN_EPS, RMS_EPS, NORM_EPS = 1e-5, 1e-6, 1e-6

SHORT = {"allow_slow_non_contiguous": True}

C_ID, C_GM, C_BD, C_EYE, C_POW, C_END = 0, 128, 192, 196, 228, 244


def shape_constants():
    c = np.zeros((P, C_END), np.float32)
    p = np.arange(P)
    j = (p % CH)[:, None]
    i = np.arange(CH)[None, :]
    c[:, C_ID:C_GM] = np.eye(P)
    c[:, C_GM:C_GM + 32] = -1.0 * (j < i)
    c[:, C_GM + 32:C_BD] = j <= i
    c[:, C_BD:C_EYE] = (p // 32)[:, None] == np.arange(4)
    c[:, C_EYE:C_POW] = j == i
    c[:, C_POW:C_POW + 8] = -0.5
    c[:, C_POW + 8:C_END] = 0.5
    return c


class Lane:

    def __init__(self, sem):
        self.sem, self.count, self.work, self.waited = sem, 0, [], {}

    def do(self, issue, *waits):
        self.wait(*waits)
        self.count += 1
        self.work.append(("do", issue, None))
        return self.sem, self.count

    def wait(self, *waits):
        for w in waits:
            if w is None:
                continue
            if isinstance(w, list):
                self.wait(*w)
                continue
            sem, value = w
            if self.waited.get(id(sem), 0) < value:
                self.waited[id(sem)] = value
                self.work.append(("wait", sem, value))

    def dma(self, box, out, src, *waits, **kw):
        self.wait(*waits)
        box.count += 16
        self.work.append(("dma", (out, src, kw), box.sem))
        return box.sem, box.count

    def run(self, eng):
        for kind, what, arg in self.work:
            if kind == "wait":
                eng.wait_ge(what, arg)
            elif kind == "do":
                what(eng).then_inc(self.sem, 1)
            else:
                out, src, kw = what
                eng.dma_start(out, src, **kw).then_inc(arg, 16)


class Box:

    def __init__(self, sem):
        self.sem, self.count = sem, 0


def macaron(nc, a, consts, out, x1_d, z_d, heads_d, beta_d, lt_d):
    T = a["L0_attn_x"].shape[1]
    NT, NS = T // TOK, T // SUP
    x_v = a["L0_attn_x"].rearrange("a (t b p) d -> (a t) p b d", b=NB, p=P)
    out_v = out.rearrange("a (t b p) d -> (a t) p b d", b=NB, p=P)
    x1_v = x1_d.rearrange("(t b p) d -> t p b d", b=NB, p=P)
    z_v = z_d.rearrange("(t b p) d -> t p b d", b=NB, p=P)

    top = ExitStack()
    with top:
        def sem(name):
            return top.enter_context(nc.semaphore(name))

        def box(name):
            return Box(sem(name))

        pe, act, dve, pool, sp = (Lane(sem(f"s_{n}")) for n in ("pe", "act", "dve", "pool", "sp"))
        lanes = (pe, act, dve, pool, sp)

        def sbuf(stack, name, shape, dt=F32):
            return stack.enter_context(nc.sbuf_tensor(name, shape, dt))

        bank = [top.enter_context(nc.psum_tensor(f"bank{i}", [P, 512], F32)) for i in range(8)]
        bank_read = [None] * 8

        cst = sbuf(top, "cst", [P, C_END])
        win = sbuf(top, "win", [P, NF, P])
        wout = sbuf(top, "wout", [P, D])
        w1t = sbuf(top, "w1t", [P, 8])
        b1t = sbuf(top, "b1t", [P, 8])
        w2t = sbuf(top, "w2t", [P, 8])
        bint = sbuf(top, "bint", [P, 1])
        b2t = sbuf(top, "b2t", [P, 1])
        boutb = sbuf(top, "boutb", [P, D])
        ident = cst[:, C_ID:C_GM]
        gmask = cst[:, C_GM:C_BD].rearrange("p (s i) -> p s i", s=2)
        bdmask = cst[:, C_BD:C_EYE]
        eye = cst[:, C_EYE:C_POW]
        neg_half, pos_half = cst[:, C_POW:C_POW + 4], cst[:, C_POW + 8:C_POW + 9]

        d_par = box("d_par")
        W1, B1, W2 = a["L0_ffn_W1"], a["L0_ffn_b1"], a["L0_ffn_W2"]
        col = lambda v: v.rearrange("(p o) -> p o", o=1)
        row = lambda v, n: v.rearrange("(o n) -> o n", o=1).broadcast_to([P, n])
        zb2 = pool.do(lambda e: e.memset(b2t[:, :], 0.0))
        loads = [(cst[:, :], consts), (boutb[:, :], row(a["L0_ffn_bout"], D))]
        for h in range(2):
            r = slice(64 * h, 64 * h + 64)
            loads += [(win[:, :, r], a["L0_ffn_Win"].rearrange("(k p) m -> p k m", p=P)),
                      (wout[r, :], a["L0_ffn_Wout"]),
                      (w1t[r, :], W1[:, 8 * h:8 * h + 8]), (b1t[r, :], B1[:, 8 * h:8 * h + 8]),
                      (w2t[r, :], W2[:, 8 * h:8 * h + 8]), (bint[r, :], col(a["L0_ffn_bin_"]))]
        loads.append((b2t[0:64, :], col(a["L0_ffn_b2"])))
        for o, s in loads:
            par = sp.dma(d_par, o, s, zb2)
        half_w = act.do(lambda e: e.activation(wout[:, :], wout[:, :], ACT.Copy, scale=0.5), par)
        half_b = act.do(lambda e: e.activation(boutb[:, :], boutb[:, :], ACT.Copy, scale=0.5), par)
        fold = dve.do(lambda e: e.scalar_tensor_tensor(b1t[:, :], w1t[:, :], bint[:, 0:1], b1t[:, :],
                                                       ALU.mult, ALU.add), par)
        ready = [par, half_w, half_b, fold]

        def layernorm(buf, stats, mv, rs, nm, got, freed):
            def bn(e):
                for b in range(NB):
                    r = e.bn_stats(stats[:, b, :], buf[:, b, :])
                return r

            def ag(e):
                for b in range(NB):
                    r = e.bn_aggr(mv[:, b, :], stats[:, b, :])
                return r
            t = dve.do(bn, got)
            t = dve.do(ag, t, freed)
            t = pool.do(lambda e: e.tensor_scalar(rs[:, :], mv[:, :, 1], LN_EPS, None, ALU.add), t, freed)
            t_rs = pool.do(lambda e: e.tensor_tensor(rs[:, :], rs[:, :], neg_half, ALU.pow), t)
            t_nm = dve.do(lambda e: e.scalar_tensor_tensor(nm[:, :], mv[:, :, 0], -1.0, rs[:, :],
                                                           ALU.mult, ALU.mult), t_rs)
            return t_nm

        def apply_norm(dst, src, rs, nm, got, freed):
            return [act.do(lambda e, b=b: e.activation(dst[:, b, :], src[:, b, :], ACT.Identity,
                                                       bias=nm[:, b:b + 1], scale=rs[:, b:b + 1]),
                           got, freed) for b in range(NB)]

        def turn(src, f, bk, got):
            def go(e):
                for b in range(NB):
                    r = e.transpose(bank[bk][:, b * P:(b + 1) * P], src[:, b, f * P:(f + 1) * P], ident)
                return r
            return pe.do(go, got, par, bank_read[bk])

        def hidden(xT, got, bk, relu, g, g_free):
            def mm(e):
                for f in range(NF):
                    r = e.matmul(bank[bk][:, :], win[:, f, :], xT[:, f, :], start=f == 0, stop=f == NF - 1)
                return r
            s = pe.do(mm, got, ready, bank_read[bk])
            acc = g_free
            for h in range(8):
                rb = relu[h % 2]
                t = act.do(lambda e, h=h, rb=rb: e.activation(rb["t"][:, :], bank[bk][:, :], ACT.Relu,
                                                              bias=b1t[:, h:h + 1], scale=w1t[:, h:h + 1]),
                           s, rb["read"], ready)
                if h == 0:
                    acc = dve.do(lambda e, rb=rb: e.tensor_scalar(g[:, :], rb["t"][:, :], w2t[:, 0:1],
                                                                  b2t[:, 0:1], ALU.mult, ALU.add), t, acc)
                else:
                    acc = dve.do(lambda e, h=h, rb=rb: e.scalar_tensor_tensor(
                        g[:, :], rb["t"][:, :], w2t[:, h:h + 1], g[:, :], ALU.mult, ALU.add), t, acc)
                rb["read"] = acc
            bank_read[bk] = t
            return s, acc

        def ffn_out(g, got, buf, base, banks):
            done = []
            for b in range(NB):
                bk = banks[b % len(banks)]
                m = pe.do(lambda e, b=b, bk=bk: e.matmul(bank[bk][:, :], g[:, b * P:(b + 1) * P], wout[:, :],
                                                         start=True, stop=True), got, bank_read[bk])
                t = dve.do(lambda e, b=b, bk=bk: e.tensor_tensor(buf[:, b, :], bank[bk][:, :], buf[:, b, :],
                                                                 ALU.add), m, base)
                bank_read[bk] = t
                done.append(t)
            return done, m

        def add_row(buf, rowt, got):
            return [pool.do(lambda e, b=b: e.tensor_tensor(buf[:, b, :], buf[:, b, :], rowt[:, :], ALU.add),
                            got) for b in range(NB)]

        def load_split(pieces, stage, d_stage):
            last = []
            free = [None, None]
            for i, (src, hi, lo) in enumerate(pieces):
                s = stage[i % 2]
                n = hi.shape[-1]
                t = sp.dma(d_stage[i % 2], s[:, 0:n], src, free[i % 2])
                th = act.do(lambda e, s=s, hi=hi, n=n: e.activation(hi, s[:, 0:n], ACT.Copy), t)
                tl = dve.do(lambda e, s=s, hi=hi, lo=lo, n=n: e.tensor_tensor(lo, s[:, 0:n], hi, ALU.subtract),
                            th)
                free[i % 2] = tl
                last = [th, tl]
            return last

        def product(e, o, lhs, rhs, first, last):
            e.matmul(o, lhs[0], rhs[0], start=first, stop=False)
            e.matmul(o, lhs[0], rhs[1], start=False, stop=False)
            return e.matmul(o, lhs[1], rhs[0], start=False, stop=last)

        def flat(v):
            return v.rearrange("p u j -> p (u j)")

        def bd_build(lane, dst, src, n, *waits):
            return lane.do(lambda e: e.tensor_tensor(
                dst, src.unsqueeze(2).broadcast_to([P, n, 4, CH]),
                bdmask.unsqueeze(1).unsqueeze(3).broadcast_to([P, n, 4, CH]), ALU.mult), *waits)

        def barrier():
            now = [(ln.sem, ln.count) for ln in (pe, act, dve, pool) if ln.count]
            for ln in lanes:
                ln.wait(now)

        kinds = ("k", "q", "v")

        def projections():
            with ExitStack() as st:
                wp = {}
                hb = sbuf(st, "hb", [P, 5, TU, CH])
                rawk = sbuf(st, "rawk", [P, TU, CH])
                kbuf = sbuf(st, "kbuf", [P, TU, CH])
                kt = hb[:, KT1, :, :]
                ltb = sbuf(st, "ltb", [P, TU, CH])
                bs = sbuf(st, "bs", [P, TC, CH])
                bg = sbuf(st, "bg", [P, TC, GROUPS])
                nrm = sbuf(st, "nrm", [P, TU])
                rn = sbuf(st, "rn", [P, TU])
                bdk = [sbuf(st, f"bdk{i}", [P, 4, 4, CH]) for i in range(2)]
                stage = [flat(b[:, 0:TC, :]) for b in (kbuf, ltb)]
                d_stage = [box(f"d_stage{i}") for i in range(2)]
                pieces = []
                for n in kinds:
                    w = sbuf(st, f"w{n}_hi", [P, NF, D], F32R), sbuf(st, f"w{n}_lo", [P, NF, D], F32R)
                    wp[n] = w
                    pieces += [(a[f"L0_attn_w{n}"][k * P:(k + 1) * P, :], w[0][:, k, :], w[1][:, k, :])
                               for k in range(NF)]
                wbeta = rawk[:, 0:TC, :].rearrange("p (k x) c -> p k (x c)", k=NF)
                wb = sbuf(st, "wb_hi", [P, NF, P], F32R), sbuf(st, "wb_lo", [P, NF, P], F32R)
                bias = {n: sbuf(st, f"b{n}", [P, GROUPS]) for n in kinds}
                bbeta = sbuf(st, "bbeta", [P, 1])
                ln1 = sbuf(st, "ln1", [P, NF])
                d_w = box("d_w")
                z1 = pool.do(lambda e: e.memset(wbeta, 0.0))
                z2 = pool.do(lambda e: e.memset(bbeta[:, :], 0.0))
                wbraw = sbuf(st, "wbraw", [P, NF, HEADS])
                tw = sp.dma(d_w, wbraw[:, :, :], a["L0_attn_wbeta"].rearrange("(k p) h -> p k h", p=P), z2)
                for h in range(4):
                    tw = sp.dma(d_w, bbeta[32 * h:32 * h + GROUPS, :],
                                a["L0_attn_bbeta"].rearrange("(g h o) -> h g o", h=4, o=1)[h], **SHORT)
                for n in kinds:
                    tw = sp.dma(d_w, bias[n][:, :], a[f"L0_attn_b{n}"].rearrange("(g p) -> p g", p=P), **SHORT)
                tw = sp.dma(d_w, ln1[:, :], a["L0_attn_ln1_scale"].rearrange("(g p) -> p g", p=P), **SHORT)
                for h in range(4):
                    z1 = dve.do(lambda e, h=h: e.tensor_copy(wbeta[:, :, 32 * h:32 * h + GROUPS],
                                                             wbraw[:, :, h:HEADS:4]), tw, z1)
                t = act.do(lambda e: e.activation(wb[0][:, :, :], wbeta, ACT.Copy), z1)
                t2 = dve.do(lambda e: e.tensor_tensor(wb[1][:, :, :], wbeta, wb[0][:, :, :], ALU.subtract), t)
                w_ready = load_split(pieces, stage, d_stage) + [t, t2, tw]

                X = [sbuf(st, f"X{i}", [P, NB, D]) for i in range(2)]
                Y = [sbuf(st, f"Y{i}", [P, NB, D]) for i in range(2)]
                xT = sbuf(st, "xT", [P, NF, TOK])
                hT = sbuf(st, "hT_hi", [P, NF, TOK], F32R), sbuf(st, "hT_lo", [P, NF, TOK], F32R)
                relu = [dict(t=sbuf(st, f"relu{i}", [P, TOK]), read=None) for i in range(2)]
                g = [sbuf(st, f"g{i}", [P, TOK]) for i in range(2)]
                stats = sbuf(st, "stats", [P, NB, 6])
                mv = [sbuf(st, f"mv{i}", [P, NB, 2]) for i in range(2)]
                rs = [sbuf(st, f"rs{i}", [P, NB]) for i in range(2)]
                nm = [sbuf(st, f"nm{i}", [P, NB]) for i in range(2)]
                ri = sbuf(st, "ri", [P, NB])
                proj = [sbuf(st, f"proj{i}", [P, TOK]) for i in range(2)]
                d_x = [box(f"d_x{i}") for i in range(2)]
                d_x1 = [box(f"d_x1{i}") for i in range(2)]
                d_beta, d_lt = box("d_beta"), box("d_lt")
                d_hb = [box(f"d_hb{i}") for i in range(2)]
                T1 = {}
                x1_stored = [None, None]
                proj_read = [None, None]
                stored = {}

                def front(t):
                    i = t % 2
                    got = sp.dma(d_x[i], X[i][:, :, :], x_v[t], x1_stored[i])
                    tn = layernorm(X[i], stats, mv[0], rs[0], nm[0], got, T1.get(("xn", t - 1)))
                    xn = apply_norm(Y[i], X[i], rs[0], nm[0], tn, T1.get(("hturn", t - 2)))
                    T1["xn", t] = xn
                    T1["xb", t] = add_row(X[i], boutb, [xn, half_b])

                def turn_x(t):
                    i, xn, free = t % 2, T1["xn", t], T1.get(("win", t - 1))
                    ends = []
                    for f in range(NF):
                        bk = 3 + f % 2
                        m = turn(Y[i], f, bk, xn)
                        e_ = act.do(lambda e, f=f, bk=bk: e.activation(xT[:, f, :], bank[bk][:, :], ACT.Copy), m, free)
                        bank_read[bk] = e_
                        ends.append(e_)
                    T1["xT", t], T1["xturn", t] = ends, m

                def s2(t):
                    i = t % 2
                    s, acc = hidden(xT, T1["xT", t], 5, relu, g[i], T1.get(("wout", t - 2)))
                    T1["win", t], T1["g", t] = s, acc

                def s3(t):
                    i = t % 2
                    x1, m = ffn_out(g[i], T1["g", t], X[i], T1["xb", t], (6, 7))
                    T1["wout", t] = m
                    tn = layernorm(X[i], stats, mv[1], rs[1], nm[1], x1, T1.get(("h", t - 1)))
                    q = dve.do(lambda e: e.tensor_tensor(ri[:, :], rs[1][:, :], rs[1][:, :], ALU.mult), tn,
                               T1.get(("h", t - 1)))
                    q = dve.do(lambda e: e.tensor_tensor(ri[:, :], ri[:, :], mv[1][:, :, 1], ALU.mult), q)
                    q = dve.do(lambda e: e.tensor_scalar(ri[:, :], ri[:, :], RMS_EPS, None, ALU.add), q)
                    q = pool.do(lambda e: e.tensor_tensor(ri[:, :], ri[:, :], neg_half, ALU.pow), q)
                    y = apply_norm(Y[i], X[i], rs[1], nm[1], tn, T1["xturn", t])
                    h = []
                    for b in range(NB):
                        h.append(dve.do(lambda e, b=b: e.tensor_scalar(Y[i][:, b, :], Y[i][:, b, :], ri[:, b:b + 1],
                                                                       None, ALU.mult), y, q))
                    T1["h", t] = h
                    x1_stored[i] = sp.dma(d_x1[i], x1_v[t], X[i][:, :, :], x1)
                    T1["x1read", t] = y
                    x1_stored[i] = [x1_stored[i], y]

                def s4(t):
                    i = t % 2
                    hi, lo = hT
                    free = T1.get(("proj", t - 1))
                    ends = []
                    for f in range(NF):
                        bk = 3 + f % 2
                        m = turn(Y[i], f, bk, T1["h", t])
                        th = act.do(lambda e, f=f, bk=bk: e.activation(hi[:, f, :], bank[bk][:, :], ACT.Copy,
                                                                       scale=ln1[:, f:f + 1]), m, free, tw)
                        tl = dve.do(lambda e, f=f, bk=bk: e.scalar_tensor_tensor(
                            lo[:, f, :], bank[bk][:, :], ln1[:, f:f + 1], hi[:, f, :], ALU.mult, ALU.subtract),
                            m, th, free)
                        bank_read[bk] = tl
                        ends.append(tl)
                    T1["hT", t], T1["hturn", t] = ends, m

                def product_of(t, n):
                    bk, slot = n % 3, n % 2
                    kind, g4 = ("b", 0) if n == 0 else ("kvq"[(n - 1) // 4], (n - 1) % 4)
                    w = wb if kind == "b" else wp[kind]
                    c = slice(g4 * P, (g4 + 1) * P)

                    def mm(e):
                        for f in range(NF):
                            r = product(e, bank[bk][:, :], (w[0][:, f, c], w[1][:, f, c]),
                                        (hT[0][:, f, :], hT[1][:, f, :]), f == 0, f == NF - 1)
                        return r
                    m = pe.do(mm, T1["hT", t], w_ready, bank_read[bk])
                    T1["proj", t] = m
                    units = slice(g4 * TC, (g4 + 1) * TC)
                    dst, free = {"b": (proj[slot][:, :], proj_read[slot]),
                                 "v": (proj[slot][:, :], proj_read[slot]),
                                 "k": (flat(rawk[:, units, :]), T1.get(("gram", t - 1))),
                                 "q": (flat(hb[:, Q1, units, :]), [stored.get("q"), T1.get(("gram", t - 1))])}[kind]
                    ev = act.do(lambda e: e.activation(
                        dst, bank[bk][:, :], ACT.Sigmoid if kind == "b" else ACT.Identity,
                        bias=bbeta[:, 0:1] if kind == "b" else bias[kind][:, g4:g4 + 1]), m, free)
                    bank_read[bk] = ev
                    if kind == "b":
                        q = dve.do(lambda e: e.transpose(bs[:, :, :].rearrange("p c g -> p (c g)"), proj[slot][:, :]),
                                   ev, T1.get(("kb", t - 1)), T1.get("bg"))
                        proj_read[slot] = q
                        T1["bs", t] = q
                        q = pool.do(lambda e: e.tensor_copy(bg[:, :, :], bs[:, :, 0:GROUPS]), q, stored.get("b"))
                        T1["bg"] = q
                        stored["b"] = sp.dma(d_beta, beta_d[t], bg[:, :, :], q)
                    elif kind == "v":
                        proj_read[slot] = dve.do(lambda e: e.transpose(flat(hb[:, V1, units, :]), proj[slot][:, :]),
                                                 ev, stored.get("v"))
                        T1["v", t] = proj_read[slot]
                    elif kind == "k":
                        T1["k", t] = ev
                    else:
                        T1["q", t] = ev

                def prepare(t):
                    K = hb[:, K1, :, :]
                    q = dve.do(lambda e: e.transpose(flat(K), flat(rawk[:, :, :])), T1["k", t], stored.get("v"),
                               T1.get(("gram", t - 1)), T1.get(("kT", t - 1)), T1.get(("kb", t - 1)))
                    sq = act.do(lambda e: e.activation(kbuf[:, :, :], K, ACT.Square), q, T1.get(("kbT", t - 1)),
                                w_ready)
                    q = dve.do(lambda e: e.tensor_reduce(nrm[:, :], kbuf[:, :, :], AX.X, ALU.add), sq)
                    q = pool.do(lambda e: e.tensor_tensor(nrm[:, :], nrm[:, :], pos_half.broadcast_to([P, TU]),
                                                          ALU.pow), q)
                    q = dve.do(lambda e: e.tensor_scalar(nrm[:, :], nrm[:, :], NORM_EPS, None, ALU.add), q)
                    q = dve.do(lambda e: e.reciprocal(rn[:, :], nrm[:, :]), q)
                    kn = dve.do(lambda e: e.tensor_tensor(K, K, rn[:, :].unsqueeze(2).broadcast_to([P, TU, HD]),
                                                          ALU.mult), q)
                    kb = pool.do(lambda e: e.tensor_tensor(
                        kbuf[:, :, :].rearrange("p (g c) j -> p g c j", g=GROUPS),
                        K.rearrange("p (g c) j -> p g c j", g=GROUPS),
                        bs[:, :, 0:GROUPS].rearrange("p c g -> p g c").unsqueeze(3)
                        .broadcast_to([P, GROUPS, TC, HD]), ALU.mult), kn, T1["bs", t])
                    T1["kb", t] = kb
                    T1["kn", t] = kn
                    T1["kT", t] = dve.do(lambda e: e.transpose(flat(kt), flat(K)), kn,
                                         T1.get(("gram", t - 1)))

                def turn_bk(t):
                    T1["kbT", t] = dve.do(lambda e: e.transpose(flat(rawk[:, :, :]), flat(kbuf[:, :, :])),
                                          T1["kb", t])

                def gram(t, u):
                    k = (u // 4) % 2
                    bk = 6 + k
                    tbd = bd_build(pool, bdk[k][:, :, :, :], rawk[:, u:u + 4, :], 4, T1["kbT", t],
                                   T1.get(("bdk", k)))

                    def mm(e):
                        for n in range(4):
                            r = e.matmul(bank[bk][:, n * WIDE:(n + 1) * WIDE].rearrange("p (s i) -> p s i", s=3),
                                         bdk[k][:, n, :, :].rearrange("p h j -> p (h j)"),
                                         hb[:, K1:KT1 + 1, u + n, :], start=True, stop=True)
                        return r
                    m = pe.do(mm, tbd, T1["kT", t], T1["q", t], bank_read[bk])
                    T1["bdk", k] = m
                    gb = bank[bk][:, 0:4 * WIDE].rearrange("p (u s i) -> p u s i", s=3, i=CH)
                    t1 = dve.do(lambda e: e.tensor_tensor(
                        ltb[:, u:u + 4, :], gb[:, :, 2, :], gmask[:, 0:1, :].broadcast_to([P, 4, CH]), ALU.mult),
                        m, stored.get("lt"))
                    t2 = dve.do(lambda e: e.tensor_tensor(
                        hb[:, P1, u:u + 4, :], gb[:, :, 1, :], gmask[:, 1:2, :].broadcast_to([P, 4, CH]),
                        ALU.mult), m, stored.get("pv"))
                    bank_read[bk] = [t1, t2]
                    if u == TU - 4:
                        T1["gram", t] = m
                        stored["lt"] = sp.dma(d_lt, lt_d[t // 2, :, :, (t % 2) * TC:(t % 2 + 1) * TC, :],
                                              ltb[:, :, :].rearrange("p (g c) i -> p g c i", g=GROUPS), t1)
                        stored["pv"] = sp.dma(d_hb[0], heads_d[t, :, P1, :, :], hb[:, P1, :, :], t2)

                def store_rest(t):
                    t_ = sp.dma(d_hb[1], heads_d[t, :, V1:Q1 + 1, :, :], hb[:, V1:Q1 + 1, :, :], T1["v", t],
                                T1["kn", t], T1["q", t])
                    stored["v"] = stored["q"] = t_

                front(0)
                turn_x(0)
                s2(0)
                s3(0)
                front(1)
                s4(0)
                turn_x(1)
                s2(1)
                for t in range(NT + 1):
                    now, more, prev = t < NT, t + 1 < NT, t > 0
                    grams = [(lambda u=u: gram(t - 1, u)) for u in range(0, TU, 4)] if prev else []

                    def some(n):
                        for _ in range(n):
                            if grams:
                                grams.pop(0)()
                    if now:
                        product_of(t, 0)
                        product_of(t, 5)
                    some(4)
                    if more:
                        s3(t + 1)
                    for n in (6, 7, 8):
                        if now:
                            product_of(t, n)
                        some(4)
                    if now:
                        for n in (1, 2, 3, 4):
                            product_of(t, n)
                        prepare(t)
                    if t + 2 < NT:
                        front(t + 2)
                    if now:
                        for n in (9, 10, 11, 12):
                            product_of(t, n)
                        store_rest(t)
                    if more:
                        s4(t + 1)
                    if now:
                        turn_bk(t)
                    if t + 2 < NT:
                        turn_x(t + 2)
                        s2(t + 2)
                return [stored["b"], stored["lt"], stored["pv"], stored["v"], x1_stored]

        stored1 = projections()
        barrier()
        for ln in lanes:
            ln.wait(stored1)

        def delta():
            with ExitStack() as st:
                wo = sbuf(st, "wo", [P, NF, D])
                bo = sbuf(st, "bo", [P, D])
                hd = [sbuf(st, f"hd{i}", [P, 5, TU, CH]) for i in range(2)]
                bg = [sbuf(st, f"bg2{i}", [P, TC, GROUPS]) for i in range(2)]
                lt = [sbuf(st, f"lt{i}", [P, NU, CH]) for i in range(2)]
                sysb = sbuf(st, "sysb", [P, CH, 4, CH])
                tmp = sbuf(st, "tmp", [P, 4 * 16 * 15])
                bdn = [sbuf(st, f"bdn{i}", [P, 4, 4, CH]) for i in range(2)]
                bdur = [sbuf(st, f"bdur{i}", [P, 4, 2, 4, CH]) for i in range(2)]
                ur = [sbuf(st, f"ur{i}", [P, 4, 2, HD]) for i in range(2)]
                op = [sbuf(st, f"op{i}", [P, 4, 2, HD]) for i in range(2)]
                gt = [sbuf(st, f"gt{i}", [P, 4, CH]) for i in range(2)]
                psi = [sbuf(st, f"psi{i}", [P, 4, HD]) for i in range(2)]
                fi = [sbuf(st, f"fi{i}", [P, 4, HD]) for i in range(2)]
                sT = [sbuf(st, f"sT{i}", [P, 4, HD]) for i in range(2)]
                oT = [sbuf(st, f"oT{i}", [P, GROUPS, P]) for i in range(2)]
                x1b = [sbuf(st, f"x1b{i}", [P, D]) for i in range(2)]
                zb = [sbuf(st, f"zb{i}", [P, D]) for i in range(2)]
                stat2 = [sbuf(st, f"stat2{i}", [P, 6]) for i in range(2)]
                mv2 = [sbuf(st, f"mv2{i}", [P, 2]) for i in range(2)]
                rs2 = [sbuf(st, f"rs2{i}", [P, 1]) for i in range(2)]
                nm2 = [sbuf(st, f"nm2{i}", [P, 1]) for i in range(2)]
                d_wo = box("d_wo")
                d_hd = [box(f"d_hd{i}") for i in range(2)]
                d_ltl = [box(f"d_ltl{i}") for i in range(2)]
                d_x1b = [box(f"d_x1b{i}") for i in range(2)]
                d_z = [box(f"d_z{i}") for i in range(2)]
                two = sp.dma(d_wo, wo[:, :, :], a["L0_attn_wo"].rearrange("(k p) n -> p k n", p=P))
                two = sp.dma(d_wo, bo[:, :], row(a["L0_attn_bo"], D))
                state = dve.do(lambda e: e.memset(sT[0][:, :, :], 0.0))
                E = {}


                def load_tile(t):
                    i = t % 2
                    free = E.get(("tile", t - 2))
                    sp.dma(d_hd[i], hd[i][:, P2:Q2 + 1, :, :], heads_d[t], free)
                    got = sp.dma(d_hd[i], bg[i][:, :, :], beta_d[t], E.get(("hd", t - 2)))
                    kb = pool.do(lambda e: e.tensor_tensor(
                        hd[i][:, B2, :, :].rearrange("p (g c) j -> p g c j", g=GROUPS),
                        hd[i][:, K2, :, :].rearrange("p (g c) j -> p g c j", g=GROUPS),
                        bg[i][:, :, :].rearrange("p c g -> p g c").unsqueeze(3)
                        .broadcast_to([P, GROUPS, TC, HD]), ALU.mult), got, free)
                    E["hd", t] = [got, kb]

                def solver(s):
                    L = lt[s % 2]
                    got = sp.dma(d_ltl[s % 2], L[:, :, :].rearrange("p (g c) i -> p g c i", g=GROUPS), lt_d[s],
                                 E.get(("lt", s - 2)))
                    for i4 in range(0, CH, 4):
                        bk = 2 + (i4 // 4) % 2

                        def go(e, i4=i4, bk=bk):
                            for n in range(4):
                                r = e.transpose(bank[bk][:, n * P:(n + 1) * P], L[:, :, i4 + n], ident)
                            return r
                        m = pe.do(go, got, bank_read[bk])
                        ev = act.do(lambda e, i4=i4, bk=bk: e.activation(
                            sysb[:, i4:i4 + 4, :, :].rearrange("p i h j -> p (i h j)"), bank[bk][:, :], ACT.Copy),
                            m, E.get("back"))
                        bank_read[bk] = ev
                        yield
                    t = ev
                    N = sysb[:, :, :, :].rearrange("p i h j -> p h i j")
                    for j in range(1, CH - 1):
                        rows = CH - 1 - j
                        tt = tmp[:, 0:4 * rows * j].rearrange("p (h i k) -> p h i k", h=4, i=rows)
                        t = dve.do(lambda e, j=j, rows=rows, tt=tt: e.tensor_tensor(
                            tt, N[:, :, j + 1:CH, j:j + 1].broadcast_to([P, 4, rows, j]),
                            N[:, :, j:j + 1, 0:j].broadcast_to([P, 4, rows, j]), ALU.mult), t)
                        yield
                        t = dve.do(lambda e, j=j, tt=tt: e.tensor_tensor(
                            N[:, :, j + 1:CH, 0:j], N[:, :, j + 1:CH, 0:j], tt, ALU.add), t)
                        yield
                    for i4 in range(0, CH, 4):
                        bk = 2 + (i4 // 4) % 2

                        def back(e, i4=i4, bk=bk):
                            for n in range(4):
                                r = e.transpose(bank[bk][:, n * P:(n + 1) * P],
                                                sysb[:, i4 + n, :, :].rearrange("p h j -> p (h j)"), ident)
                            return r
                        m = pe.do(back, t, bank_read[bk])
                        ev = act.do(lambda e, i4=i4, bk=bk: e.activation(
                            L[:, :, i4:i4 + 4].rearrange("p u i -> p i u"),
                            bank[bk][:, :].rearrange("p (i u) -> p i u", i=4), ACT.Copy), m)
                        bank_read[bk] = ev
                        yield
                    E["back"] = m
                    E["nt", s] = ev

                def unit(b, c, n):
                    return b.rearrange("p (g c) j -> p g c j", g=GROUPS)[:, :, c % n, :]

                def lhs(b):
                    return b.rearrange("p h j -> p (h j)")

                UR, OUT_U, OUT_R = 4, 5, 1

                def wide(bk, n):
                    return bank[bk][:, n * WIDE:(n + 1) * WIDE].rearrange("p (s j) -> p s j", s=3)

                def narrow(bk):
                    return bank[bk][:, 0:4 * WIDE].rearrange("p (g s j) -> p g s j", g=4, s=3)

                def products(c):
                    s, k, h = c // NC, c % 2, hd[(c // TC) % 2]
                    n_bd = bd_build(pool, bdn[k][:, :, :, :], unit(lt[s % 2][:, :, :], c, NC), 4, E["nt", s],
                                    E.get(("bdn", k)))

                    def mm(e):
                        for n in range(4):
                            r = e.matmul(wide(UR, n), lhs(bdn[k][:, n, :, :]),
                                         h[:, V2:Q2 + 1, n * TC + c % TC, :],
                                         start=True, stop=True)
                        return r
                    E["lt", s] = n_bd
                    m = pe.do(mm, n_bd, bank_read[UR], E["hd", c // TC])
                    E["bdn", k] = m
                    ps = narrow(UR)
                    t = [dve.do(lambda e, w=w: e.tensor_tensor(ur[k][:, :, w, :], ps[:, :, w, :],
                                                               unit(h[:, V2 + w, :, :], c, TC), ALU.add),
                                m, E.get(("bdur", k))) for w in range(2)]
                    bank_read[UR] = t
                    E["bdur", k] = dve.do(lambda e: e.tensor_tensor(
                        bdur[k][:, :, :, :, :].rearrange("p g s h j -> p (g s) h j"),
                        ur[k][:, :, :, :].rearrange("p g s j -> p (g s) j").unsqueeze(2)
                        .broadcast_to([P, 8, 4, CH]),
                        bdmask.unsqueeze(1).unsqueeze(3).broadcast_to([P, 8, 4, CH]), ALU.mult),
                        t, E.get(("out", k)))

                def within(c):
                    k, h = c % 2, hd[(c // TC) % 2]

                    def mm(w, bk):
                        def go(e):
                            for n in range(4):
                                r = e.matmul(wide(bk, n), lhs(bdur[k][:, n, w, :, :]),
                                             h[:, B2:V2 + 1, n * TC + c % TC, :], start=True, stop=True)
                            return r
                        return pe.do(go, E["bdur", k], E["hd", c // TC], bank_read[bk])
                    m_r = mm(1, OUT_R)
                    m_u = mm(0, OUT_U)
                    E["out", k] = m_u
                    pu, pr = narrow(OUT_U), narrow(OUT_R)
                    tf = dve.do(lambda e: e.tensor_tensor(
                        fi[k][:, :, :], eye.unsqueeze(1).broadcast_to([P, 4, HD]), pr[:, :, B2, :],
                        ALU.subtract), m_r, E.get(("step", k)))
                    tg = dve.do(lambda e: e.tensor_tensor(gt[k][:, :, :], unit(h[:, Q2, :, :], c, TC),
                                                          pr[:, :, P2, :], ALU.subtract),
                                m_r, E.get(("sg", k)))
                    bank_read[OUT_R] = [tg, tf]
                    to = act.do(lambda e: e.activation(op[k][:, :, :, :], pu[:, :, B2:P2 + 1, :], ACT.Copy),
                                m_u, E.get(("o", k)), E.get(("psi", k)))
                    bank_read[OUT_U] = to
                    E["op", k], E["gt", k], E["fi", k] = to, tg, tf
                    E["psi", k] = dve.do(lambda e: e.transpose(psi[k][:, :, :], op[k][:, :, B2, :]), to,
                                         E.get(("st", k)))
                    E["tile", c // TC] = [m_u, tg]

                def tiles(e, bk, lhsT, rhs):
                    for n in range(4):
                        for h in range(4):
                            r = slice(32 * h, 32 * h + 32)
                            i = e.matmul(bank[bk][r, n * 32:(n + 1) * 32], lhsT[r, n, :], rhs[r, n, :],
                                         start=True, stop=True)
                    return i

                def across(c):
                    k, o2 = c % 2, (c // 4) % 2
                    m_s = pe.do(lambda e: tiles(e, 6, fi[k], sT[k]), E["fi", k], E["state"], bank_read[6])
                    E["step", k] = m_s
                    state = dve.do(lambda e: e.tensor_tensor(
                        sT[1 - k][:, :, :], bank[6][:, 0:P].rearrange("p (g d) -> p g d", g=4),
                        psi[k][:, :, :], ALU.add), m_s, E["psi", k], E.get(("sg", 1 - k)))
                    bank_read[6] = state
                    m_g = pe.do(lambda e: tiles(e, 7, sT[k], gt[k]), E["state"], E["gt", k], bank_read[7])
                    E["st", k], E["state"] = state, state
                    E["sg", k] = m_g
                    t_o = dve.do(lambda e: e.tensor_tensor(
                        oT[o2][:, :, (c % 4) * CH:(c % 4 + 1) * CH],
                        bank[7][:, 0:P].rearrange("p (g d) -> p g d", g=4),
                        op[k][:, :, P2, :], ALU.add), m_g, E["op", k], E.get(("wo", o2)) if c % 4 == 0 else None)
                    bank_read[7] = t_o
                    E["o", k], E["oT", o2] = t_o, t_o

                def residual(blk):
                    o2 = blk % 2
                    tx = sp.dma(d_x1b[o2], x1b[o2][:, :], x1_d[blk * P:(blk + 1) * P, :], E.get(("y", o2)))
                    q = dve.do(lambda e: e.bn_stats(stat2[o2][:, :], x1b[o2][:, :]), tx)
                    q = dve.do(lambda e: e.bn_aggr(mv2[o2][:, :], stat2[o2][:, :]), q, E.get(("y", o2)))
                    q = pool.do(lambda e: e.tensor_scalar(rs2[o2][:, :], mv2[o2][:, 1:2], LN_EPS, None,
                                                          ALU.add), q, E.get(("y", o2)))
                    q = pool.do(lambda e: e.tensor_tensor(rs2[o2][:, :], rs2[o2][:, :], neg_half[:, 0:1],
                                                          ALU.pow), q)
                    q = dve.do(lambda e: e.scalar_tensor_tensor(
                        nm2[o2][:, :], mv2[o2][:, 0:1], -1.0, rs2[o2][:, :], ALU.mult, ALU.mult), q)
                    y = act.do(lambda e: e.activation(zb[o2][:, :], x1b[o2][:, :], ACT.Identity,
                                                      bias=nm2[o2][:, 0:1], scale=rs2[o2][:, 0:1]),
                               q, E.get(("z", o2)))
                    E["y", o2] = y
                    E["yb", o2] = pool.do(lambda e: e.tensor_tensor(zb[o2][:, :], zb[o2][:, :], bo[:, :],
                                                                    ALU.add), y, two)

                def out_product(blk):
                    o2, bk = blk % 2, 0

                    def mm(e):
                        for f in range(NF):
                            r = e.matmul(bank[bk][:, :], oT[o2][:, f, :], wo[:, f, :], start=f == 0,
                                         stop=f == NF - 1)
                        return r
                    m = pe.do(mm, E["oT", o2], two, bank_read[bk])
                    E["wo", o2] = m
                    t = dve.do(lambda e: e.tensor_tensor(zb[o2][:, :], bank[bk][:, :], zb[o2][:, :], ALU.add),
                               m, E["yb", o2])
                    bank_read[bk] = t
                    E["z", o2] = sp.dma(d_z[o2], z_d[blk * P:(blk + 1) * P, :], zb[o2][:, :], t)

                E["state"] = state
                load_tile(0)
                for _ in solver(0):
                    pass
                load_tile(1)
                steps = iter(())
                chunks = NS * NC
                for c in range(chunks + 3):
                    if c < chunks:
                        if c % NC == 0 and c // NC + 1 < NS:
                            steps = solver(c // NC + 1)
                        if c % NC == NC - 1:
                            for _ in steps:
                                pass
                    if c >= 2 and c - 2 < chunks:
                        across(c - 2)
                    if c < chunks:
                        products(c)
                    for _, _ in zip(range(3), steps):
                        pass
                    if 1 <= c <= chunks:
                        within(c - 1)
                    if c >= 2 and (c - 2) % TC == 0 and 2 <= (c - 2) // TC + 1 < NT:
                        load_tile((c - 2) // TC + 1)
                    if c % 4 == 0 and c < chunks:
                        residual(c // 4)
                    if c % 4 == 2 and c > 4:
                        out_product((c - 6) // 4)
                return [E["z", 0], E["z", 1]]

        stored2 = delta()
        barrier()
        for ln in lanes:
            ln.wait(stored2)

        def dense():
            with ExitStack() as st:
                w1 = sbuf(st, "w1_hi", [P, NF, DFF], F32R), sbuf(st, "w1_lo", [P, NF, DFF], F32R)
                w2 = sbuf(st, "w2_hi", [P, NM, D], F32R), sbuf(st, "w2_lo", [P, NM, D], F32R)
                b1m = sbuf(st, "b1m", [P, NM])
                ln2 = sbuf(st, "ln2", [P, NF])
                b2b = sbuf(st, "b2b", [P, D])
                hT = sbuf(st, "h2_hi", [P, NF, TOK], F32R), sbuf(st, "h2_lo", [P, NF, TOK], F32R)
                xT = sbuf(st, "x2T", [P, NF, TOK])
                Z = sbuf(st, "Z", [P, NB, D])
                S = sbuf(st, "S", [P, NB, D])
                H = sbuf(st, "H", [P, NB, D])
                gl = [sbuf(st, f"gl{i}", [P, TOK]) for i in range(2)]
                gh = [(sbuf(st, f"gh{i}", [P, TOK], F32R), sbuf(st, f"glo{i}", [P, TOK], F32R)) for i in range(2)]
                g = sbuf(st, "g3", [P, TOK])
                stats = sbuf(st, "stats3", [P, NB, 6])
                mv = sbuf(st, "mv3", [P, NB, 2])
                rs = sbuf(st, "rs3", [P, NB])
                nm = sbuf(st, "nm3", [P, NB])
                ss = sbuf(st, "ss3", [P, NB])
                relu = [dict(t=sbuf(st, f"relu3{i}", [P, TOK]), read=None) for i in range(1)] * 2
                d_w = box("d_w3")
                d_Z, d_S, d_out = box("d_Z"), box("d_S"), box("d_out")
                tw = sp.dma(d_w, b1m[:, :], a["L0_attn_b1"].rearrange("(g p) -> p g", p=P), **SHORT)
                tw = sp.dma(d_w, ln2[:, :], a["L0_attn_ln2_scale"].rearrange("(g p) -> p g", p=P), **SHORT)
                tw = sp.dma(d_w, b2b[:, :], row(a["L0_attn_b2"], D))
                pieces = []
                for k in range(NF):
                    for n in range(4):
                        c = slice(n * D, (n + 1) * D)
                        pieces.append((a["L0_attn_w1"][k * P:(k + 1) * P, c], w1[0][:, k, c], w1[1][:, k, c]))
                for m in range(NM):
                    pieces.append((a["L0_attn_w2"][m * P:(m + 1) * P, :], w2[0][:, m, :], w2[1][:, m, :]))
                d_st3 = [box("d_st3a"), box("d_st3b")]
                w_ready = load_split(pieces, [xT[:, 0, :], xT[:, 1, :]], d_st3) + [tw]
                R = {}

                def front(t):
                    got = sp.dma(d_Z, Z[:, :, :], z_v[t], R.get("s"), R.get("hs"))

                    def sq(e):
                        for b in range(NB):
                            r = e.activation(H[:, b, :], Z[:, b, :], ACT.Square, accum_out=ss[:, b:b + 1])
                        return r
                    q = act.do(sq, got, R.get("xturn"), R.get("hs"))
                    q = dve.do(lambda e: e.tensor_scalar(ss[:, :], ss[:, :], 1.0 / D, RMS_EPS, ALU.mult, ALU.add), q)
                    q = pool.do(lambda e: e.tensor_tensor(ss[:, :], ss[:, :], neg_half, ALU.pow), q)
                    h = [dve.do(lambda e, b=b: e.tensor_scalar(H[:, b, :], Z[:, b, :], ss[:, b:b + 1], None,
                                                               ALU.mult), q) for b in range(NB)]
                    R["hs"] = h
                    for f in range(NF):
                        bk = 6 + f % 2
                        m = turn(H, f, bk, h)
                        th = act.do(lambda e, f=f, bk=bk: e.activation(hT[0][:, f, :], bank[bk][:, :], ACT.Copy,
                                                                       scale=ln2[:, f:f + 1]), m, R.get("w1"), tw)
                        tl = dve.do(lambda e, f=f, bk=bk: e.scalar_tensor_tensor(
                            hT[1][:, f, :], bank[bk][:, :], ln2[:, f:f + 1], hT[0][:, f, :], ALU.mult, ALU.subtract),
                            th)
                        bank_read[bk] = tl
                    R["hT"], R["hturn"] = tl, m

                def residual(t):
                    got = sp.dma(d_S, S[:, :, :], x1_v[t], R.get("out"))
                    q = [pool.do(lambda e, b=b: e.tensor_tensor(S[:, b, :], S[:, b, :], Z[:, b, :], ALU.add), got)
                         for b in range(NB)]
                    R["s"] = q
                    R["sb"] = add_row(S, b2b, [q, tw])

                def mlp_up(m):
                    bk, k = m % 2, m % 2

                    def mm(e):
                        c = slice(m * P, (m + 1) * P)
                        for f in range(NF):
                            r = product(e, bank[bk][:, :], (w1[0][:, f, c], w1[1][:, f, c]),
                                        (hT[0][:, f, :], hT[1][:, f, :]), f == 0, f == NF - 1)
                        return r
                    t = pe.do(mm, R["hT"], w_ready, bank_read[bk])
                    R["w1"] = t
                    t = act.do(lambda e: e.activation(gl[k][:, :], bank[bk][:, :], ACT.Gelu_apprx_tanh,
                                                      bias=b1m[:, m:m + 1]), t, R.get(("gl", k)))
                    bank_read[bk] = t
                    th = act.do(lambda e: e.activation(gh[k][0][:, :], gl[k][:, :], ACT.Copy), t, R.get(("gh", k)))
                    tl = dve.do(lambda e: e.tensor_tensor(gh[k][1][:, :], gl[k][:, :], gh[k][0][:, :], ALU.subtract),
                                th, R.get(("gh", k)))
                    R["gl", k], R["up", m] = tl, tl

                def mlp_down(m):
                    k = m % 2

                    def mm(e):
                        for b in range(NB):
                            r = product(e, bank[2 + b][:, :], [x[:, b * P:(b + 1) * P] for x in gh[k]],
                                        (w2[0][:, m, :], w2[1][:, m, :]), m == 0, m == NM - 1)
                        return r
                    t = pe.do(mm, R["up", m], bank_read[2:6] if m == 0 else None)
                    R["gh", k], R["down"] = t, t

                def x2(t):
                    ends = []
                    for b in range(NB):
                        q = dve.do(lambda e, b=b: e.tensor_tensor(S[:, b, :], bank[2 + b][:, :], S[:, b, :], ALU.add),
                                   R["down"], R["sb"])
                        bank_read[2 + b] = q
                        ends.append(q)
                    R["x2"] = ends

                def ffn_front(t):
                    tn = layernorm(S, stats, mv, rs, nm, R["x2"], R.get("xn"))
                    xn = apply_norm(H, S, rs, nm, tn, [R["hturn"], R.get("xturn")])
                    R["xn"] = xn
                    R["xb"] = add_row(S, boutb, xn)
                    for f in range(NF):
                        bk = 6 + f % 2
                        m = turn(H, f, bk, xn)
                        e_ = act.do(lambda e, f=f, bk=bk: e.activation(xT[:, f, :], bank[bk][:, :], ACT.Copy), m,
                                    R.get("win"), w_ready)
                        bank_read[bk] = e_
                    R["xT"], R["xturn"] = e_, m

                def ffn_mid(t):
                    R["win"], R["g"] = hidden(xT, R["xT"], 6, relu, g, R.get("wout"))

                def ffn_end(t):
                    x3, R["wout"] = ffn_out(g, R["g"], S, R["xb"], (7,))
                    R["out"] = sp.dma(d_out, out_v[t], S[:, :, :], x3)

                front(0)
                for t in range(NT):
                    for m in range(NM):
                        mlp_up(m)
                        if m:
                            mlp_down(m - 1)
                        if t and m == 1:
                            ffn_front(t - 1)
                        if t and m == 4:
                            ffn_mid(t - 1)
                        if t and m == 9:
                            ffn_end(t - 1)
                        if m == 11:
                            residual(t)
                    if t + 1 < NT:
                        front(t + 1)
                    mlp_down(NM - 1)
                    x2(t)
                ffn_front(NT - 1)
                ffn_mid(NT - 1)
                ffn_end(NT - 1)
                return R["out"]

        stored3 = dense()
        sp.wait(stored1, stored2, stored3)

        block = top.enter_context(nc.Block())

        @block.sync
        def _(eng):
            sp.run(eng)

        @block.scalar
        def _(eng):
            act.run(eng)

        @block.vector
        def _(eng):
            dve.run(eng)

        @block.gpsimd
        def _(eng):
            pool.run(eng)

        @block.tensor
        def _(eng):
            pe.run(eng)


_INS = ['L0_attn_x', 'L0_attn_wq', 'L0_attn_bq', 'L0_attn_wk', 'L0_attn_bk', 'L0_attn_wv', 'L0_attn_bv',
        'L0_attn_wbeta', 'L0_attn_bbeta', 'L0_attn_wo', 'L0_attn_bo', 'L0_attn_w1', 'L0_attn_b1', 'L0_attn_w2',
        'L0_attn_b2', 'L0_attn_ln1_scale', 'L0_attn_ln2_scale', 'L0_ffn_Win', 'L0_ffn_bin_', 'L0_ffn_W1',
        'L0_ffn_b1', 'L0_ffn_W2', 'L0_ffn_b2', 'L0_ffn_Wout', 'L0_ffn_bout']


def kernel(**inputs):
    import numpy as _np
    import concourse.bacc as _bacc
    from concourse import mybir as _mybir
    from concourse.bass_utils import run_bass_kernel_spmd as _run

    nc = _bacc.Bacc("TRN2", target_bir_lowering=False, num_devices=1)
    f32 = _mybir.dt.float32
    arrays, args = {}, {}
    for name in _INS:
        v = _np.ascontiguousarray(inputs[name])
        arrays[f"in_{name}"] = v
        args[name] = nc.dram_tensor(f"in_{name}", v.shape, _mybir.dt.from_np(v.dtype), kind="ExternalInput").ap()
    arrays["consts"] = shape_constants()
    consts = nc.dram_tensor("consts", arrays["consts"].shape, f32, kind="ExternalInput").ap()
    shape = inputs['L0_attn_x'].shape
    T = shape[1]
    out = nc.dram_tensor("out", shape, f32, kind="ExternalOutput").ap()
    x1_d = nc.dram_tensor("x1_scratch", (T, D), f32).ap()
    z_d = nc.dram_tensor("z_scratch", (T, D), f32).ap()
    heads_d = nc.dram_tensor("heads_scratch", (T // TOK, P, 4, TU, CH), f32).ap()
    beta_d = nc.dram_tensor("beta_scratch", (T // TOK, P, TC, GROUPS), f32).ap()
    lt_d = nc.dram_tensor("lt_scratch", (T // SUP, P, GROUPS, NC, CH), f32).ap()
    macaron(nc, args, consts, out, x1_d, z_d, heads_d, beta_d, lt_d)
    r = _run(nc, [arrays], core_ids=[0])
    return r.results[0]["out"]
```

```python
import itertools
from contextlib import ExitStack

import concourse.bass as bass
import concourse.mybir as mybir
import numpy as np

F32 = mybir.dt.float32
F32R = mybir.dt.float32r
ALU = mybir.AluOpType
ACT = mybir.ActivationFunctionType
AX = mybir.AxisListType

P = 128
D = 512
NF = D // P
HEADS, HD = 16, 32
GROUPS = HEADS // 4
DFF = 2048
NM = DFF // P
TOK = 512
NB = TOK // P
SUP = 1024
CH = 32
NC = SUP // CH
NU = GROUPS * NC
TC = TOK // CH
TU = GROUPS * TC
P1, V1, K1, Q1, KT1 = range(5)
B2, P2, V2, K2, Q2 = range(5)
WIDE = 3 * CH
LN_EPS, RMS_EPS, NORM_EPS = 1e-5, 1e-6, 1e-6

SHORT = {"allow_slow_non_contiguous": True}

C_ID, C_GM, C_BD, C_EYE, C_POW, C_END = 0, 128, 192, 196, 228, 244


def shape_constants():
    c = np.zeros((P, C_END), np.float32)
    p = np.arange(P)
    j = (p % CH)[:, None]
    i = np.arange(CH)[None, :]
    c[:, C_ID:C_GM] = np.eye(P)
    c[:, C_GM:C_GM + 32] = -1.0 * (j < i)
    c[:, C_GM + 32:C_BD] = j <= i
    c[:, C_BD:C_EYE] = (p // 32)[:, None] == np.arange(4)
    c[:, C_EYE:C_POW] = j == i
    c[:, C_POW:C_POW + 8] = -0.5
    c[:, C_POW + 8:C_END] = 0.5
    return c


class Lane:

    def __init__(self, sem):
        self.sem, self.count, self.work, self.waited = sem, 0, [], {}

    def do(self, issue, *waits):
        self.wait(*waits)
        self.count += 1
        self.work.append(("do", issue, None))
        return self.sem, self.count

    def wait(self, *waits):
        for w in waits:
            if w is None:
                continue
            if isinstance(w, list):
                self.wait(*w)
                continue
            sem, value = w
            if self.waited.get(id(sem), 0) < value:
                self.waited[id(sem)] = value
                self.work.append(("wait", sem, value))

    def dma(self, box, out, src, *waits, **kw):
        self.wait(*waits)
        box.count += 16
        self.work.append(("dma", (out, src, kw), box.sem))
        return box.sem, box.count

    def run(self, eng):
        for kind, what, arg in self.work:
            if kind == "wait":
                eng.wait_ge(what, arg)
            elif kind == "do":
                what(eng).then_inc(self.sem, 1)
            else:
                out, src, kw = what
                eng.dma_start(out, src, **kw).then_inc(arg, 16)


class Box:

    def __init__(self, sem):
        self.sem, self.count = sem, 0


def macaron(nc, a, consts, out, x1_d, z_d, heads_d, beta_d, lt_d):
    T = a["L0_attn_x"].shape[1]
    NT, NS = T // TOK, T // SUP
    x_v = a["L0_attn_x"].rearrange("a (t b p) d -> (a t) p b d", b=NB, p=P)
    out_v = out.rearrange("a (t b p) d -> (a t) p b d", b=NB, p=P)
    x1_v = x1_d.rearrange("(t b p) d -> t p b d", b=NB, p=P)
    z_v = z_d.rearrange("(t b p) d -> t p b d", b=NB, p=P)

    top = ExitStack()
    with top:
        def sem(name):
            return top.enter_context(nc.semaphore(name))

        def box(name):
            return Box(sem(name))

        pe, act, dve, pool, sp = (Lane(sem(f"s_{n}")) for n in ("pe", "act", "dve", "pool", "sp"))
        lanes = (pe, act, dve, pool, sp)

        def sbuf(stack, name, shape, dt=F32):
            return stack.enter_context(nc.sbuf_tensor(name, shape, dt))

        bank = [top.enter_context(nc.psum_tensor(f"bank{i}", [P, 512], F32)) for i in range(8)]
        bank_read = [None] * 8

        cst = sbuf(top, "cst", [P, C_END])
        win = sbuf(top, "win", [P, NF, P])
        wout = sbuf(top, "wout", [P, D])
        w1t = sbuf(top, "w1t", [P, 8])
        b1t = sbuf(top, "b1t", [P, 8])
        w2t = sbuf(top, "w2t", [P, 8])
        bint = sbuf(top, "bint", [P, 1])
        b2t = sbuf(top, "b2t", [P, 1])
        boutb = sbuf(top, "boutb", [P, D])
        ident = cst[:, C_ID:C_GM]
        gmask = cst[:, C_GM:C_BD].rearrange("p (s i) -> p s i", s=2)
        bdmask = cst[:, C_BD:C_EYE]
        eye = cst[:, C_EYE:C_POW]
        neg_half, pos_half = cst[:, C_POW:C_POW + 4], cst[:, C_POW + 8:C_POW + 9]

        d_par = box("d_par")
        W1, B1, W2 = a["L0_ffn_W1"], a["L0_ffn_b1"], a["L0_ffn_W2"]
        col = lambda v: v.rearrange("(p o) -> p o", o=1)
        row = lambda v, n: v.rearrange("(o n) -> o n", o=1).broadcast_to([P, n])
        zb2 = pool.do(lambda e: e.memset(b2t[:, :], 0.0))
        loads = [(cst[:, :], consts), (boutb[:, :], row(a["L0_ffn_bout"], D))]
        for h in range(2):
            r = slice(64 * h, 64 * h + 64)
            loads += [(win[:, :, r], a["L0_ffn_Win"].rearrange("(k p) m -> p k m", p=P)),
                      (wout[r, :], a["L0_ffn_Wout"]),
                      (w1t[r, :], W1[:, 8 * h:8 * h + 8]), (b1t[r, :], B1[:, 8 * h:8 * h + 8]),
                      (w2t[r, :], W2[:, 8 * h:8 * h + 8]), (bint[r, :], col(a["L0_ffn_bin_"]))]
        loads.append((b2t[0:64, :], col(a["L0_ffn_b2"])))
        for o, s in loads:
            par = sp.dma(d_par, o, s, zb2)
        half_w = act.do(lambda e: e.activation(wout[:, :], wout[:, :], ACT.Copy, scale=0.5), par)
        half_b = act.do(lambda e: e.activation(boutb[:, :], boutb[:, :], ACT.Copy, scale=0.5), par)
        fold = dve.do(lambda e: e.scalar_tensor_tensor(b1t[:, :], w1t[:, :], bint[:, 0:1], b1t[:, :],
                                                       ALU.mult, ALU.add), par)
        ready = [par, half_w, half_b, fold]

        def layernorm(buf, stats, mv, rs, nm, got, freed):
            for b in range(NB):
                t = dve.do(lambda e, b=b: e.bn_stats(stats[:, b, :], buf[:, b, :]), got)
                if b == 1:
                    yield

            def ag(e):
                for b in range(NB):
                    r = e.bn_aggr(mv[:, b, :], stats[:, b, :])
                return r
            t = dve.do(ag, t, freed)
            t = pool.do(lambda e: e.tensor_scalar(rs[:, :], mv[:, :, 1], LN_EPS, None, ALU.add), t, freed)
            t_rs = pool.do(lambda e: e.tensor_tensor(rs[:, :], rs[:, :], neg_half, ALU.pow), t)
            yield
            return dve.do(lambda e: e.scalar_tensor_tensor(nm[:, :], mv[:, :, 0], -1.0, rs[:, :],
                                                           ALU.mult, ALU.mult), t_rs)

        def apply_norm(dst, src, rs, nm, got, freed):
            return [act.do(lambda e, b=b: e.activation(dst[:, b, :], src[:, b, :], ACT.Identity,
                                                       bias=nm[:, b:b + 1], scale=rs[:, b:b + 1]),
                           got, freed) for b in range(NB)]

        def apply_norm_block(dst, src, rs, nm, b, got, freed):
            return act.do(lambda e: e.activation(dst[:, b, :], src[:, b, :], ACT.Identity, bias=nm[:, b:b + 1],
                                                 scale=rs[:, b:b + 1]), got, freed)

        def turn(src, f, bk, got):
            def go(e):
                for b in range(NB):
                    r = e.transpose(bank[bk][:, b * P:(b + 1) * P], src[:, b, f * P:(f + 1) * P], ident)
                return r
            return pe.do(go, got, par, bank_read[bk])

        def hidden(xT, got, bk, relu, g, g_free, R, key, pace=2):
            def mm(e):
                for f in range(NF):
                    r = e.matmul(bank[bk][:, :], win[:, f, :], xT[:, f, :], start=f == 0, stop=f == NF - 1)
                return r
            R["win", key] = s = pe.do(mm, got, ready, bank_read[bk])
            acc = g_free
            for h in range(8):
                rb = relu[h % 2]
                t = act.do(lambda e, h=h, rb=rb: e.activation(rb["t"][:, :], bank[bk][:, :], ACT.Relu,
                                                              bias=b1t[:, h:h + 1], scale=w1t[:, h:h + 1]),
                           s, rb["read"], ready)
                if h == 0:
                    acc = dve.do(lambda e, rb=rb: e.tensor_scalar(g[:, :], rb["t"][:, :], w2t[:, 0:1],
                                                                  b2t[:, 0:1], ALU.mult, ALU.add), t, acc)
                else:
                    acc = dve.do(lambda e, h=h, rb=rb: e.scalar_tensor_tensor(
                        g[:, :], rb["t"][:, :], w2t[:, h:h + 1], g[:, :], ALU.mult, ALU.add), t, acc)
                rb["read"] = acc
                bank_read[bk] = t
                R["g", key] = acc
                if h % pace == pace - 1:
                    yield

        def ffn_out(g, got, buf, base, banks):
            done = []
            for b in range(NB):
                bk = banks[b % len(banks)]
                m = pe.do(lambda e, b=b, bk=bk: e.matmul(bank[bk][:, :], g[:, b * P:(b + 1) * P], wout[:, :],
                                                         start=True, stop=True), got, bank_read[bk])
                t = dve.do(lambda e, b=b, bk=bk: e.tensor_tensor(buf[:, b, :], bank[bk][:, :], buf[:, b, :],
                                                                 ALU.add), m, base)
                bank_read[bk] = t
                done.append(t)
            return done, m

        def add_row(buf, rowt, got):
            return [pool.do(lambda e, b=b: e.tensor_tensor(buf[:, b, :], buf[:, b, :], rowt[:, :], ALU.add),
                            got) for b in range(NB)]

        def load_split(pieces, stage, d_stage):
            ends = []
            free = [None] * len(stage)
            for i, (src, hi, lo) in enumerate(pieces):
                j = i % len(stage)
                s = stage[j]
                t = sp.dma(d_stage[j], s, src, free[j])
                th = act.do(lambda e, s=s, hi=hi: e.activation(hi, s, ACT.Copy), t)
                tl = dve.do(lambda e, s=s, hi=hi, lo=lo: e.tensor_tensor(lo, s, hi, ALU.subtract), th)
                free[j] = tl
                ends.append([th, tl])
            return ends

        def product(e, o, lhs, rhs, first, last):
            e.matmul(o, lhs[0], rhs[0], start=first, stop=False)
            e.matmul(o, lhs[0], rhs[1], start=False, stop=False)
            return e.matmul(o, lhs[1], rhs[0], start=False, stop=last)

        def flat(v):
            return v.rearrange("p u j -> p (u j)")

        def bd_build(lane, dst, src, n, *waits):
            return lane.do(lambda e: e.tensor_tensor(
                dst, src.unsqueeze(2).broadcast_to([P, n, 4, CH]),
                bdmask.unsqueeze(1).unsqueeze(3).broadcast_to([P, n, 4, CH]), ALU.mult), *waits)

        def bd_build_act(lane, dst, src, n, *waits):
            def go(e):
                for h in range(4):
                    r = e.activation(dst[:, :, h, :], src, ACT.Copy, scale=bdmask[:, h:h + 1])
                return r
            return lane.do(go, *waits)

        def barrier():
            now = [(ln.sem, ln.count) for ln in (pe, act, dve, pool) if ln.count]
            for ln in lanes:
                ln.wait(now)

        kinds = ("v", "q", "k")

        def projections():
            with ExitStack() as st:
                wp = {}
                hb = sbuf(st, "hb", [P, 5, TU, CH])
                rawk = sbuf(st, "rawk", [P, TU, CH])
                kbuf = sbuf(st, "kbuf", [P, TU, CH])
                kt = hb[:, KT1, :, :]
                ltb = sbuf(st, "ltb", [P, TU, CH])
                bs = sbuf(st, "bs", [P, TC, CH])
                bg = [sbuf(st, f"bg{i}", [P, TC, GROUPS]) for i in range(2)]
                nrm = sbuf(st, "nrm", [P, TU])
                rn = sbuf(st, "rn", [P, TU])
                bdk = [sbuf(st, f"bdk{i}", [P, 4, 4, CH]) for i in range(4)]
                stage = [flat(b[:, n * TC:(n + 1) * TC, :]) for b in (kbuf, ltb) for n in range(GROUPS)]
                d_stage = [box(f"d_stage{i}") for i in range(len(stage))]
                pieces = []
                for n in kinds:
                    w = sbuf(st, f"w{n}_hi", [P, NF, D], F32R), sbuf(st, f"w{n}_lo", [P, NF, D], F32R)
                    wp[n] = w
                    pieces += [(a[f"L0_attn_w{n}"][k * P:(k + 1) * P, :], w[0][:, k, :], w[1][:, k, :])
                               for k in range(NF)]
                wbeta = rawk[:, 0:TC, :].rearrange("p (k x) c -> p k (x c)", k=NF)
                wb = sbuf(st, "wb_hi", [P, NF, P], F32R), sbuf(st, "wb_lo", [P, NF, P], F32R)
                bias = {n: sbuf(st, f"b{n}", [P, GROUPS]) for n in kinds}
                bbeta = sbuf(st, "bbeta", [P, 1])
                ln1 = sbuf(st, "ln1", [P, NF])
                d_w = box("d_w")
                z1 = pool.do(lambda e: e.memset(wbeta, 0.0))
                z2 = pool.do(lambda e: e.memset(bbeta[:, :], 0.0))
                wbraw = sbuf(st, "wbraw", [P, NF, HEADS])
                tw = sp.dma(d_w, wbraw[:, :, :], a["L0_attn_wbeta"].rearrange("(k p) h -> p k h", p=P), z2)
                for h in range(4):
                    tw = sp.dma(d_w, bbeta[32 * h:32 * h + GROUPS, :],
                                a["L0_attn_bbeta"].rearrange("(g h o) -> h g o", h=4, o=1)[h], **SHORT)
                for n in kinds:
                    tw = sp.dma(d_w, bias[n][:, :], a[f"L0_attn_b{n}"].rearrange("(g p) -> p g", p=P), **SHORT)
                tw = sp.dma(d_w, ln1[:, :], a["L0_attn_ln1_scale"].rearrange("(g p) -> p g", p=P), **SHORT)
                for h in range(4):
                    z1 = dve.do(lambda e, h=h: e.tensor_copy(wbeta[:, :, 32 * h:32 * h + GROUPS],
                                                             wbraw[:, :, h:HEADS:4]), tw, z1)
                t = act.do(lambda e: e.activation(wb[0][:, :, :], wbeta, ACT.Copy), z1)
                t2 = dve.do(lambda e: e.tensor_tensor(wb[1][:, :, :], wbeta, wb[0][:, :, :], ALU.subtract), t)
                split = load_split(pieces, stage, d_stage)
                w_ready = {n: split[i * NF:(i + 1) * NF] + [tw] for i, n in enumerate(kinds)}
                w_ready["b"] = [t, t2, tw]

                X = [sbuf(st, f"X{i}", [P, NB, D]) for i in range(2)]
                Y = [sbuf(st, f"Y{i}", [P, NB, D]) for i in range(2)]
                xT = sbuf(st, "xT", [P, NF, TOK])
                hT = sbuf(st, "hT_hi", [P, NF, TOK], F32R), sbuf(st, "hT_lo", [P, NF, TOK], F32R)
                relu = [dict(t=sbuf(st, f"relu{i}", [P, TOK]), read=None) for i in range(2)]
                g = [sbuf(st, f"g{i}", [P, TOK]) for i in range(2)]
                stats = [sbuf(st, f"stats{i}", [P, NB, 6]) for i in range(2)]
                mv = [sbuf(st, f"mv{i}", [P, NB, 2]) for i in range(2)]
                rs = [sbuf(st, f"rs{i}", [P, NB]) for i in range(2)]
                nm = [sbuf(st, f"nm{i}", [P, NB]) for i in range(2)]
                ri = sbuf(st, "ri", [P, NB])
                proj = [sbuf(st, f"proj{i}", [P, TOK]) for i in range(2)]
                d_x = [box(f"d_x{i}") for i in range(2)]
                d_x1 = [box(f"d_x1{i}") for i in range(2)]
                d_beta = [box(f"d_beta{i}") for i in range(2)]
                d_hb = {(n, g4): box(f"d_hb_{n}{g4}") for n in ("p", "v", "k", "q", "lt") for g4 in range(GROUPS)}
                T1 = {}
                x1_stored = [None, None]
                proj_read = [None, None]
                stored = {}

                def front(t):
                    i = t % 2
                    got = sp.dma(d_x[i], X[i][:, :, :], x_v[t], x1_stored[i])
                    yield
                    tn = yield from layernorm(X[i], stats[0], mv[0], rs[0], nm[0], got, T1.get(("xn", t - 1)))
                    xn, xb = [], []
                    for b in range(NB):
                        xn += [apply_norm_block(Y[i], X[i], rs[0], nm[0], b, tn, T1.get(("hturn", t - 2)))]
                        xb += [dve.do(lambda e, b=b: e.tensor_tensor(X[i][:, b, :], X[i][:, b, :], boutb[:, :],
                                                                     ALU.add), xn[-1], half_b)]
                        T1["xn", t], T1["xb", t] = xn, xb
                        yield

                turn_banks = itertools.cycle((3, 4, 5))

                def turn_x(t, f):
                    i, bk = t % 2, next(turn_banks)
                    T1["xturn", t] = m = turn(Y[i], f, bk, T1["xn", t])
                    T1["xT", t] = bank_read[bk] = act.do(
                        lambda e: e.activation(xT[:, f, :], bank[bk][:, :], ACT.Copy), m, T1.get(("win", t - 1)))

                def s2(t):
                    return hidden(xT, T1["xT", t], next(turn_banks), relu, g[t % 2], T1.get(("wout", t - 2)), T1, t)

                def s3(t):
                    i = t % 2
                    x1, m = ffn_out(g[i], T1["g", t], X[i], T1["xb", t], (6, 7))
                    T1["wout", t] = m
                    yield
                    x1_stored[i] = sp.dma(d_x1[i], x1_v[t], X[i][:, :, :], x1)
                    tn = yield from layernorm(X[i], stats[1], mv[1], rs[1], nm[1], x1, T1.get(("h", t - 1)))
                    q = dve.do(lambda e: e.tensor_tensor(ri[:, :], rs[1][:, :], rs[1][:, :], ALU.mult), tn,
                               T1.get(("h", t - 1)))
                    q = dve.do(lambda e: e.tensor_tensor(ri[:, :], ri[:, :], mv[1][:, :, 1], ALU.mult), q)
                    q = dve.do(lambda e: e.tensor_scalar(ri[:, :], ri[:, :], RMS_EPS, None, ALU.add), q)
                    q = pool.do(lambda e: e.tensor_tensor(ri[:, :], ri[:, :], neg_half, ALU.pow), q)
                    yield
                    h, y = [], []
                    for b in range(NB):
                        y.append(apply_norm_block(Y[i], X[i], rs[1], nm[1], b, tn, T1["xturn", t]))
                        h.append(dve.do(lambda e, b=b: e.tensor_scalar(Y[i][:, b, :], Y[i][:, b, :], ri[:, b:b + 1],
                                                                       None, ALU.mult), y, q))
                        if b % 2:
                            yield
                    T1["h", t] = h
                    x1_stored[i] = [x1_stored[i], y]

                def turn_h(t, f):
                    hi, lo = hT
                    bk, free = next(turn_banks), T1.get(("proj", t - 1))
                    T1["hturn", t] = m = turn(Y[t % 2], f, bk, T1["h", t])
                    th = act.do(lambda e: e.activation(hi[:, f, :], bank[bk][:, :], ACT.Copy,
                                                       scale=ln1[:, f:f + 1]), m, free, tw)
                    T1["hT", t, f] = bank_read[bk] = dve.do(lambda e: e.scalar_tensor_tensor(
                        lo[:, f, :], bank[bk][:, :], ln1[:, f:f + 1], hi[:, f, :], ALU.mult, ALU.subtract),
                        m, th, free)

                def units(g4):
                    return slice(g4 * TC, (g4 + 1) * TC)

                turns = iter(range(1 << 30))

                def product_of(t, kind, g4=0):
                    n = next(turns)
                    bk, slot = n % 3, n % 2
                    w = wb if kind == "b" else wp[kind]
                    c = slice(g4 * P, (g4 + 1) * P)

                    for f in range(NF):
                        m = pe.do(lambda e, f=f: product(e, bank[bk][:, :], (w[0][:, f, c], w[1][:, f, c]),
                                                         (hT[0][:, f, :], hT[1][:, f, :]), f == 0, f == NF - 1),
                                  T1["hT", t, f], w_ready[kind], bank_read[bk] if f == 0 else None)
                    T1["proj", t] = m
                    u = units(g4)
                    dst, free = {"b": (proj[slot][:, :], proj_read[slot]),
                                 "v": (proj[slot][:, :], proj_read[slot]),
                                 "k": (flat(rawk[:, u, :]), T1.get(("bd", t - 1, g4))),
                                 "q": (flat(hb[:, Q1, u, :]), [stored.get(("q", g4)), T1.get(("gram", t - 1, g4))])}[kind]
                    ev = act.do(lambda e: e.activation(
                        dst, bank[bk][:, :], ACT.Sigmoid if kind == "b" else ACT.Identity,
                        bias=bbeta[:, 0:1] if kind == "b" else bias[kind][:, g4:g4 + 1]), m, free)
                    bank_read[bk] = ev
                    if kind == "b":
                        q = dve.do(lambda e: e.transpose(bs[:, :, :].rearrange("p c g -> p (c g)"), proj[slot][:, :]),
                                   ev, T1.get(("bg", t - 1)))
                        proj_read[slot] = q
                        q = pool.do(lambda e: e.tensor_copy(bg[t % 2][:, :, :], bs[:, :, 0:GROUPS]), q,
                                    stored.get(("b", t % 2)), T1.get(("kb", t - 2)))
                        T1["bg", t] = q
                        stored["b", t % 2] = sp.dma(d_beta[t % 2], beta_d[t], bg[t % 2][:, :, :], q)
                    elif kind == "v":
                        proj_read[slot] = dve.do(lambda e: e.transpose(flat(hb[:, V1, u, :]), proj[slot][:, :]),
                                                 ev, stored.get(("v", g4)))
                        store(t, "v", V1, g4, proj_read[slot])
                    elif kind == "q":
                        T1["q", t, g4] = ev
                        store(t, "q", Q1, g4, ev)
                    else:
                        T1["k", t, g4] = ev

                def store(t, kind, slot, g4, got):
                    u = units(g4)
                    stored[kind, g4] = sp.dma(d_hb[kind, g4], heads_d[t, :, slot, u, :], hb[:, slot, u, :], got)

                def prepare(t, g4):
                    u = units(g4)
                    K = hb[:, K1, u, :]
                    q = dve.do(lambda e: e.transpose(flat(K), flat(rawk[:, u, :])), T1["k", t, g4],
                               stored.get(("k", g4)), T1.get(("gram", t - 1, g4)))
                    yield
                    sq = act.do(lambda e: e.activation(kbuf[:, u, :], K, ACT.Square), q,
                                T1.get(("kbT", t - 1, g4)), split)
                    yield
                    q = dve.do(lambda e: e.tensor_reduce(nrm[:, u], kbuf[:, u, :], AX.X, ALU.add), sq)
                    q = pool.do(lambda e: e.tensor_tensor(nrm[:, u], nrm[:, u], pos_half.broadcast_to([P, TC]),
                                                          ALU.pow), q)
                    yield
                    yield
                    q = dve.do(lambda e: e.tensor_scalar(nrm[:, u], nrm[:, u], NORM_EPS, None, ALU.add), q)
                    q = dve.do(lambda e: e.reciprocal(rn[:, u], nrm[:, u]), q)
                    kn = dve.do(lambda e: e.tensor_tensor(K, K, rn[:, u].unsqueeze(2).broadcast_to([P, TC, HD]),
                                                          ALU.mult), q)
                    T1["kb", t] = kb = pool.do(lambda e: e.tensor_tensor(
                        kbuf[:, u, :], K, bg[t % 2][:, :, g4:g4 + 1].broadcast_to([P, TC, HD]), ALU.mult), kn,
                        T1["bg", t])
                    T1["kT", t, g4] = dve.do(lambda e: e.transpose(flat(hb[:, KT1, u, :]), flat(K)), kn)
                    store(t, "k", K1, g4, kn)
                    yield
                    yield
                    T1["kbT", t, g4] = dve.do(lambda e: e.transpose(flat(rawk[:, u, :]), flat(kbuf[:, u, :])), kb)
                    yield

                def spread(t, g4):
                    finish(prep[t, g4])
                    for u in range(g4 * TC, (g4 + 1) * TC, 4):
                        spread_four(t, u)

                def spread_four(t, u):
                    k = (u // 4) % 4
                    build, lane = (bd_build, pool) if k % 2 else (bd_build_act, act)
                    T1["bd", t, u // TC] = T1["bdk", k] = build(
                        lane, bdk[k][:, :, :, :], rawk[:, u:u + 4, :], 4, T1["kbT", t, u // TC],
                        T1.get(("bdu", k)))

                def gram(t, u):
                    k, g4 = (u // 4) % 4, u // TC
                    bk = 6 + k % 2

                    def mm(e):
                        for n in range(4):
                            r = e.matmul(bank[bk][:, n * WIDE:(n + 1) * WIDE].rearrange("p (s i) -> p s i", s=3),
                                         bdk[k][:, n, :, :].rearrange("p h j -> p (h j)"),
                                         hb[:, K1:KT1 + 1, u + n, :], start=True, stop=True)
                        return r
                    m = pe.do(mm, T1["bdk", k], T1["kT", t, g4], T1["q", t, g4], bank_read[bk])
                    T1["bdu", k] = m
                    gb = bank[bk][:, 0:4 * WIDE].rearrange("p (u s i) -> p u s i", s=3, i=CH)
                    t1 = dve.do(lambda e: e.tensor_tensor(
                        ltb[:, u:u + 4, :], gb[:, :, 2, :], gmask[:, 0:1, :].broadcast_to([P, 4, CH]), ALU.mult),
                        m, stored.get(("lt", g4)))
                    t2 = dve.do(lambda e: e.tensor_tensor(
                        hb[:, P1, u:u + 4, :], gb[:, :, 1, :], gmask[:, 1:2, :].broadcast_to([P, 4, CH]),
                        ALU.mult), m, stored.get(("p", g4)))
                    bank_read[bk] = [t1, t2]
                    T1["gram", t, g4] = m
                    if u % TC == TC - 4:
                        stored["lt", g4] = sp.dma(d_hb["lt", g4], lt_d[t // 2, :, g4, (t % 2) * TC:(t % 2 + 1) * TC, :],
                                                  ltb[:, units(g4), :], t1)
                        store(t, "p", P1, g4, t2)

                def finish(*chains):
                    for c in chains:
                        for _ in c:
                            pass

                for t in (0, 1):
                    finish(front(t))
                    for f in range(NF):
                        turn_x(t, f)
                    if t == 0:
                        finish(s2(0), s3(0))
                        for f in range(NF):
                            turn_h(0, f)
                chains = [s2(1)]
                prep = {}

                def tick():
                    for c in list(chains):
                        if next(c, 0) == 0:
                            chains.remove(c)

                def project(t, kind, g4=0):
                    product_of(t, kind, g4)
                    if kind == "k":
                        prep[t, g4] = prepare(t, g4)
                        chains.append(prep[t, g4])
                    tick()

                def grams(t, u, n):
                    for m in range(n):
                        gram(t, u + 4 * m)

                for t in range(NT):
                    project(t, "b")
                    if 1 <= t < NT - 1:
                        chains.append(s2(t + 1))
                    project(t, "v", 0)
                    project(t, "q", 0)
                    if t:
                        spread(t - 1, 1)
                    project(t, "k", 0)
                    if t + 1 < NT:
                        x1_chain = s3(t + 1)
                    if t + 2 < NT:
                        x_chain = front(t + 2)
                        chains.append(x_chain)
                    for g4 in range(1, GROUPS):
                        if t:
                            grams(t - 1, g4 * TC, 2)
                        project(t, "v", g4)
                        if g4 == 1 and t + 1 < NT:
                            chains.append(x1_chain)
                        if t:
                            grams(t - 1, g4 * TC + 8, 2)
                            if g4 + 1 < GROUPS:
                                spread(t - 1, g4 + 1)
                        project(t, "q", g4)
                        project(t, "k", g4)
                    if t + 1 < NT:
                        finish(x1_chain)
                    if t + 2 < NT:
                        finish(x_chain)
                    spread(t, 0)
                    for what, n in (("h", 0), ("h", 1), ("x", 0), ("g", 0), ("h", 2), ("g", 1), ("x", 1), ("h", 3),
                                    ("g", 2), ("x", 2), ("g", 3), ("x", 3)):
                        if what == "g":
                            gram(t, 4 * n)
                        elif what == "h" and t + 1 < NT:
                            turn_h(t + 1, n)
                        elif what == "x" and t + 2 < NT:
                            turn_x(t + 2, n)
                for g4 in range(1, GROUPS):
                    spread(NT - 1, g4)
                    grams(NT - 1, g4 * TC, 4)
                return [list(stored.values()), x1_stored]

        stored1 = projections()
        barrier()
        for ln in lanes:
            ln.wait(stored1)

        def delta():
            with ExitStack() as st:
                wo = sbuf(st, "wo", [P, NF, D])
                bo = sbuf(st, "bo", [P, D])
                hd = [sbuf(st, f"hd{i}", [P, 5, TU, CH]) for i in range(2)]
                bg = [sbuf(st, f"bg2{i}", [P, TC, GROUPS]) for i in range(2)]
                lt = [sbuf(st, f"lt{i}", [P, NU, CH]) for i in range(2)]
                sysb = sbuf(st, "sysb", [P, CH, 4, CH])
                tmp = sbuf(st, "tmp", [P, 4 * 16 * 15])
                bdn = [sbuf(st, f"bdn{i}", [P, 4, 4, CH]) for i in range(2)]
                bdu = [sbuf(st, f"bdu{i}", [P, 4, 4, CH]) for i in range(2)]
                bdr = [sbuf(st, f"bdr{i}", [P, 4, 4, CH]) for i in range(2)]
                ur = [sbuf(st, f"ur{i}", [P, 4, 2, HD]) for i in range(2)]
                op = [sbuf(st, f"op{i}", [P, 4, 2, HD]) for i in range(3)]
                gt = [sbuf(st, f"gt{i}", [P, 4, CH]) for i in range(3)]
                psi = [sbuf(st, f"psi{i}", [P, 4, HD]) for i in range(3)]
                fi = [sbuf(st, f"fi{i}", [P, 4, HD]) for i in range(3)]
                sT = [sbuf(st, f"sT{i}", [P, 4, HD]) for i in range(2)]
                oT = [sbuf(st, f"oT{i}", [P, GROUPS, P]) for i in range(2)]
                x1b = [sbuf(st, f"x1b{i}", [P, D]) for i in range(2)]
                zb = [sbuf(st, f"zb{i}", [P, D]) for i in range(2)]
                stat2 = [sbuf(st, f"stat2{i}", [P, 6]) for i in range(2)]
                mv2 = [sbuf(st, f"mv2{i}", [P, 2]) for i in range(2)]
                rs2 = [sbuf(st, f"rs2{i}", [P, 1]) for i in range(2)]
                nm2 = [sbuf(st, f"nm2{i}", [P, 1]) for i in range(2)]
                d_wo = box("d_wo")
                d_hd = [box(f"d_hd{i}") for i in range(2)]
                d_ltl = [box(f"d_ltl{i}") for i in range(2)]
                d_x1b = [box(f"d_x1b{i}") for i in range(2)]
                d_z = [box(f"d_z{i}") for i in range(2)]
                E = {}

                def load_tile(t):
                    i = t % 2
                    free = E.get(("tile", t - 2))
                    sp.dma(d_hd[i], hd[i][:, P2:Q2 + 1, :, :], heads_d[t], free)
                    got = sp.dma(d_hd[i], bg[i][:, :, :], beta_d[t], E.get(("hd", t - 2)))
                    E["hd", t] = [got]
                    yield
                    for g4 in range(GROUPS):
                        u = slice(g4 * TC, (g4 + 1) * TC)
                        E["hd", t] = [got, pool.do(lambda e, g4=g4, u=u: e.tensor_tensor(
                            hd[i][:, B2, u, :], hd[i][:, K2, u, :],
                            bg[i][:, :, g4:g4 + 1].broadcast_to([P, TC, HD]), ALU.mult), got, free)]
                        yield

                def solver(s):
                    L = lt[s % 2]
                    got = sp.dma(d_ltl[s % 2], L[:, :, :].rearrange("p (g c) i -> p g c i", g=GROUPS), lt_d[s],
                                 E.get(("lt", s - 2)))
                    yield
                    yield
                    yield
                    for i4 in range(0, CH, 4):
                        bk = 2 + (i4 // 4) % 2

                        def go(e, i4=i4, bk=bk):
                            for n in range(4):
                                r = e.transpose(bank[bk][:, n * P:(n + 1) * P], L[:, :, i4 + n], ident)
                            return r
                        m = pe.do(go, got, bank_read[bk])
                        ev = act.do(lambda e, i4=i4, bk=bk: e.activation(
                            sysb[:, i4:i4 + 4, :, :].rearrange("p i h j -> p (i h j)"), bank[bk][:, :], ACT.Copy),
                            m, E.get("back"))
                        bank_read[bk] = ev
                        yield
                    t = ev
                    N = sysb[:, :, :, :].rearrange("p i h j -> p h i j")
                    for j in range(1, CH - 1):
                        rows = CH - 1 - j
                        tt = tmp[:, 0:4 * rows * j].rearrange("p (h i k) -> p h i k", h=4, i=rows)
                        t = dve.do(lambda e, j=j, rows=rows, tt=tt: e.tensor_tensor(
                            tt, N[:, :, j + 1:CH, j:j + 1].broadcast_to([P, 4, rows, j]),
                            N[:, :, j:j + 1, 0:j].broadcast_to([P, 4, rows, j]), ALU.mult), t)
                        yield
                        t = dve.do(lambda e, j=j, tt=tt: e.tensor_tensor(
                            N[:, :, j + 1:CH, 0:j], N[:, :, j + 1:CH, 0:j], tt, ALU.add), t)
                        yield
                    for i4 in range(0, CH, 4):
                        bk = 2 + (i4 // 4) % 2

                        def back(e, i4=i4, bk=bk):
                            for n in range(4):
                                r = e.transpose(bank[bk][:, n * P:(n + 1) * P],
                                                sysb[:, i4 + n, :, :].rearrange("p h j -> p (h j)"), ident)
                            return r
                        m = pe.do(back, t, bank_read[bk])
                        ev = act.do(lambda e, i4=i4, bk=bk: e.activation(
                            L[:, :, i4:i4 + 4].rearrange("p u i -> p i u"),
                            bank[bk][:, :].rearrange("p (i u) -> p i u", i=4), ACT.Copy), m)
                        bank_read[bk] = ev
                        yield
                    E["back"] = m
                    E["nt", s] = ev

                def unit(b, c, n):
                    return b.rearrange("p (g c) j -> p g c j", g=GROUPS)[:, :, c % n, :]

                def lhs(b):
                    return b.rearrange("p h j -> p (h j)")

                UR, OUT_U, OUT_R = 4, 5, 1

                def wide(bk, n):
                    return bank[bk][:, n * WIDE:(n + 1) * WIDE].rearrange("p (s j) -> p s j", s=3)

                def narrow(bk):
                    return bank[bk][:, 0:4 * WIDE].rearrange("p (g s j) -> p g s j", g=4, s=3)

                def spread(c):
                    s, k = c // NC, c % 2
                    E["lt", s] = E["n", k] = bd_build(pool, bdn[k][:, :, :, :], unit(lt[s % 2][:, :, :], c, NC), 4,
                                                      E["nt", s], E.get(("bdn", k)))

                def products(c):
                    k, h = c % 2, hd[(c // TC) % 2]

                    def mm(e):
                        for n in range(4):
                            r = e.matmul(wide(UR, n), lhs(bdn[k][:, n, :, :]), h[:, V2:Q2 + 1, n * TC + c % TC, :],
                                         start=True, stop=True)
                        return r
                    m = pe.do(mm, E["n", k], bank_read[UR], E["hd", c // TC])
                    E["bdn", k] = m
                    t = dve.do(lambda e: e.tensor_tensor(
                        ur[k][:, :, :, :], narrow(UR)[:, :, 0:2, :],
                        h[:, V2:K2 + 1, :, :].rearrange("p s (g c) j -> p g s c j", g=GROUPS)[:, :, :, c % TC, :],
                        ALU.add), m, E.get(("bd", k)))
                    bank_read[UR] = t
                    r = bd_build(dve, bdr[k][:, :, :, :], ur[k][:, :, 1, :], 4, t, E.get(("out_r", k)))
                    u = bd_build(pool, bdu[k][:, :, :, :], ur[k][:, :, 0, :], 4, t, E.get(("out_u", k)))
                    E["bd", k] = [r, u]
                    E["bdr", k], E["bdu", k] = r, u

                def within_pe(c):
                    k, h = c % 2, hd[(c // TC) % 2]

                    def mm(bd, bk, made):
                        def go(e):
                            for n in range(4):
                                r = e.matmul(wide(bk, n), lhs(bd[k][:, n, :, :]), h[:, B2:V2 + 1, n * TC + c % TC, :],
                                             start=True, stop=True)
                            return r
                        return pe.do(go, made, E["hd", c // TC], bank_read[bk])
                    E["out_r", k] = mm(bdr, OUT_R, E["bdr", k])
                    E["out_u", k] = mm(bdu, OUT_U, E["bdu", k])

                def within_rest(c):
                    k, r, h = c % 2, c % 3, hd[(c // TC) % 2]
                    pu, pr = narrow(OUT_U), narrow(OUT_R)
                    tf = dve.do(lambda e: e.tensor_tensor(
                        fi[r][:, :, :], eye.unsqueeze(1).broadcast_to([P, 4, HD]), pr[:, :, B2, :],
                        ALU.subtract), E["out_r", k], E.get(("step", r)))
                    tg = dve.do(lambda e: e.tensor_tensor(gt[r][:, :, :], unit(h[:, Q2, :, :], c, TC),
                                                          pr[:, :, P2, :], ALU.subtract),
                                E["out_r", k], E.get(("sg", r)))
                    bank_read[OUT_R] = [tg, tf]
                    to = act.do(lambda e: e.activation(op[r][:, :, :, :], pu[:, :, B2:P2 + 1, :], ACT.Copy),
                                E["out_u", k], E.get(("o", r)), E.get(("psi", r)))
                    bank_read[OUT_U] = to
                    E["op", r], E["gt", r], E["fi", r] = to, tg, tf
                    E["tile", c // TC] = [E["out_u", k], tg]

                def turn_psi(c):
                    r = c % 3
                    E["psi", r] = dve.do(lambda e: e.transpose(psi[r][:, :, :], op[r][:, :, B2, :]), E["op", r],
                                         E.get(("st", r)))

                def tiles(e, bk, lhsT, rhs):
                    for n in range(4):
                        for h in range(4):
                            r = slice(32 * h, 32 * h + 32)
                            i = e.matmul(bank[bk][r, n * 32:(n + 1) * 32], lhsT[r, n, :], rhs[r, n, :],
                                         start=True, stop=True)
                    return i

                def step(c):
                    k, r = c % 2, c % 3
                    m = pe.do(lambda e: tiles(e, 6, fi[r], sT[k]), E["fi", r], E["state"], bank_read[6])
                    E["step", r] = m
                    E["state"] = E["st", r] = bank_read[6] = dve.do(lambda e: e.tensor_tensor(
                        sT[1 - k][:, :, :], bank[6][:, 0:P].rearrange("p (g d) -> p g d", g=4),
                        psi[r][:, :, :], ALU.add), m, E["psi", r], E.get(("sread", 1 - k)))

                def across_pe(c):
                    k, r = c % 2, c % 3
                    E["sg", r] = E["sread", k] = pe.do(lambda e: tiles(e, 7, sT[k], gt[r]), E["gt", r], bank_read[7])

                def across_rest(c):
                    r, o2 = c % 3, (c // 4) % 2
                    E["o", r] = E["oT", o2] = bank_read[7] = dve.do(lambda e: e.tensor_tensor(
                        oT[o2][:, :, (c % 4) * CH:(c % 4 + 1) * CH],
                        bank[7][:, 0:P].rearrange("p (g d) -> p g d", g=4),
                        op[r][:, :, P2, :], ALU.add), E["sg", r], E["op", r],
                        E.get(("wo", o2)) if c % 4 == 0 else None)

                def residual(blk):
                    o2 = blk % 2
                    tx = sp.dma(d_x1b[o2], x1b[o2][:, :], x1_d[blk * P:(blk + 1) * P, :], E.get(("y", o2)))
                    yield
                    q = dve.do(lambda e: e.bn_stats(stat2[o2][:, :], x1b[o2][:, :]), tx)
                    q = dve.do(lambda e: e.bn_aggr(mv2[o2][:, :], stat2[o2][:, :]), q, E.get(("y", o2)))
                    q = pool.do(lambda e: e.tensor_scalar(rs2[o2][:, :], mv2[o2][:, 1:2], LN_EPS, None,
                                                          ALU.add), q, E.get(("y", o2)))
                    q = pool.do(lambda e: e.tensor_tensor(rs2[o2][:, :], rs2[o2][:, :], neg_half[:, 0:1],
                                                          ALU.pow), q)
                    yield
                    q = dve.do(lambda e: e.scalar_tensor_tensor(
                        nm2[o2][:, :], mv2[o2][:, 0:1], -1.0, rs2[o2][:, :], ALU.mult, ALU.mult), q)
                    y = act.do(lambda e: e.activation(zb[o2][:, :], x1b[o2][:, :], ACT.Identity,
                                                      bias=nm2[o2][:, 0:1], scale=rs2[o2][:, 0:1]),
                               q, E.get(("z", o2)))
                    E["y", o2] = y
                    yield
                    E["yb", o2] = pool.do(lambda e: e.tensor_tensor(zb[o2][:, :], zb[o2][:, :], bo[:, :],
                                                                    ALU.add), y, two)
                    yield

                def out_product(blk, f):
                    o2 = blk % 2
                    m = pe.do(lambda e: e.matmul(bank[0][:, :], oT[o2][:, f, :], wo[:, f, :], start=f == 0,
                                                 stop=f == NF - 1), E["oT", o2], two, bank_read[0] if f == 0 else None)
                    if f == NF - 1:
                        E["wo", o2] = m
                        t = dve.do(lambda e: e.tensor_tensor(zb[o2][:, :], bank[0][:, :], zb[o2][:, :], ALU.add),
                                   m, E["yb", o2])
                        bank_read[0] = t
                        E["z", o2] = sp.dma(d_z[o2], z_d[blk * P:(blk + 1) * P, :], zb[o2][:, :], t)

                def advance(gen, n):
                    return sum(1 for _ in zip(range(n), gen)) == n

                first = solver(0)
                advance(first, 1)
                for _ in load_tile(0):
                    pass
                two = sp.dma(d_wo, wo[:, :, :], a["L0_attn_wo"].rearrange("(k p) n -> p k n", p=P))
                two = sp.dma(d_wo, bo[:, :], row(a["L0_attn_bo"], D))
                E["state"] = dve.do(lambda e: e.memset(sT[0][:, :, :], 0.0))
                for _ in first:
                    pass
                steps = iter(())
                ahead = load_tile(1)
                chunks = NS * NC
                spread(0)
                for c in range(chunks + 7):
                    if c % NC == 0 and c // NC + 1 < NS:
                        steps = solver(c // NC + 1)
                    if c % NC == NC - 1:
                        for _ in steps:
                            pass
                    if c % 4 == 2 and (c - 6) // 4 >= 0 and (c - 6) // 4 < chunks // 4:
                        res = residual((c - 6) // 4)
                    if 3 <= c < chunks + 3:
                        step(c - 3)
                    if c < chunks:
                        products(c)
                    if 3 <= c < chunks + 3:
                        across_pe(c - 3)
                    if 1 <= c <= chunks:
                        within_pe(c - 1)
                    if c + 1 < chunks:
                        spread(c + 1)
                    if c >= 7:
                        out_product((c - 7) // 4, (c - 7) % 4)
                    advance(steps, 2)
                    if 1 <= c <= chunks:
                        within_rest(c - 1)
                    if 3 <= c < chunks + 3:
                        across_rest(c - 3)
                    advance(steps, 1)
                    if 1 <= c <= chunks:
                        turn_psi(c - 1)
                    if c % TC == 2 and c // TC >= 1 and c // TC + 1 < NT:
                        ahead = load_tile(c // TC + 1)
                    if c % TC in (2, 8, 9, 10, 11, 12):
                        advance(ahead, 1)
                    if c >= 6:
                        advance(res, 1)
                return [E["z", 0], E["z", 1]]

        stored2 = delta()
        barrier()
        for ln in lanes:
            ln.wait(stored2)

        def dense():
            with ExitStack() as st:
                w1 = sbuf(st, "w1_hi", [P, NF, DFF], F32R), sbuf(st, "w1_lo", [P, NF, DFF], F32R)
                w2 = sbuf(st, "w2_hi", [P, NM, D], F32R), sbuf(st, "w2_lo", [P, NM, D], F32R)
                b1m = sbuf(st, "b1m", [P, NM])
                ln2 = sbuf(st, "ln2", [P, NF])
                b2b = sbuf(st, "b2b", [P, D])
                hT = sbuf(st, "h2_hi", [P, NF, TOK], F32R), sbuf(st, "h2_lo", [P, NF, TOK], F32R)
                xT = sbuf(st, "x2T", [P, NF, TOK])
                Z = [sbuf(st, f"Z{i}", [P, NB, D]) for i in range(2)]
                H = sbuf(st, "H", [P, NB, D])
                gl = [sbuf(st, f"gl{i}", [P, TOK]) for i in range(2)]
                gh = [(sbuf(st, f"gh{i}", [P, TOK], F32R), sbuf(st, f"glo{i}", [P, TOK], F32R)) for i in range(2)]
                g = sbuf(st, "g3", [P, TOK])
                stats = sbuf(st, "stats3", [P, NB, 6])
                mv = sbuf(st, "mv3", [P, NB, 2])
                rs = sbuf(st, "rs3", [P, NB])
                nm = sbuf(st, "nm3", [P, NB])
                ss = sbuf(st, "ss3", [P, NB])
                relu = [dict(t=sbuf(st, f"relu3{i}", [P, TOK]), read=None) for i in range(2)]
                d_w = box("d_w3")
                d_Z = [box(f"d_Z{i}") for i in range(2)]
                d_out = [box(f"d_out{i}") for i in range(2)]
                d_H = box("d_H")
                R = {}

                def load_z(t):
                    return sp.dma(d_Z[t % 2], Z[t % 2][:, :, :], z_v[t], R.get(("out", t - 2)))

                R["z", 0] = load_z(0)
                tw = sp.dma(d_w, b1m[:, :], a["L0_attn_b1"].rearrange("(g p) -> p g", p=P), **SHORT)
                tw = sp.dma(d_w, ln2[:, :], a["L0_attn_ln2_scale"].rearrange("(g p) -> p g", p=P), **SHORT)
                tw = sp.dma(d_w, b2b[:, :], row(a["L0_attn_b2"], D))

                def rms(t):
                    z, got = Z[t % 2], R["z", t]

                    for b in range(NB):
                        q = act.do(lambda e, b=b: e.activation(H[:, b, :], z[:, b, :], ACT.Square,
                                                               accum_out=ss[:, b:b + 1]), got, R.get("xturn"),
                                   R.get("x1z"), R.get("hs"))
                        if b == 1:
                            yield
                    q = dve.do(lambda e: e.tensor_scalar(ss[:, :], ss[:, :], 1.0 / D, RMS_EPS, ALU.mult, ALU.add), q)
                    q = pool.do(lambda e: e.tensor_tensor(ss[:, :], ss[:, :], neg_half, ALU.pow), q)
                    yield
                    R["hs"] = [dve.do(lambda e, b=b: e.tensor_scalar(H[:, b, :], z[:, b, :], ss[:, b:b + 1], None,
                                                                     ALU.mult), q) for b in range(NB)]
                    yield

                def turn_h(f):
                    bk = 6 + f % 2
                    R["hturn"] = m = turn(H, f, bk, R["hs"])
                    th = act.do(lambda e: e.activation(hT[0][:, f, :], bank[bk][:, :], ACT.Copy,
                                                       scale=ln2[:, f:f + 1]), m, R.get("up_pe"), tw)
                    R["hT", f] = bank_read[bk] = dve.do(lambda e: e.scalar_tensor_tensor(
                        hT[1][:, f, :], bank[bk][:, :], ln2[:, f:f + 1], hT[0][:, f, :], ALU.mult, ALU.subtract),
                        th, R.get("up_pe"))

                def residual(t):
                    z = Z[t % 2]
                    got = sp.dma(d_H, H[:, :, :], x1_v[t], R.get("xturn"), R["hturn"])
                    yield
                    yield
                    ends, sums = [], []
                    for b in range(NB):
                        q = pool.do(lambda e, b=b: e.tensor_tensor(z[:, b, :], z[:, b, :], H[:, b, :], ALU.add),
                                    got, R["hs"])
                        sums.append(q)
                        ends.append(pool.do(lambda e, b=b: e.tensor_tensor(z[:, b, :], z[:, b, :], b2b[:, :],
                                                                           ALU.add), q, tw))
                        R["x1z"], R["sb", t] = sums, ends
                        if b == 1:
                            yield

                def mlp_up(m):
                    bk, k = m % 2, m % 2
                    c = slice(m * P, (m + 1) * P)
                    for f in range(NF):
                        t = pe.do(lambda e, f=f: product(e, bank[bk][:, :], (w1[0][:, f, c], w1[1][:, f, c]),
                                                         (hT[0][:, f, :], hT[1][:, f, :]), f == 0, f == NF - 1),
                                  R["hT", f], w1_ready[m // 4], bank_read[bk] if f == 0 else None)
                    R["up_pe"] = t
                    t = act.do(lambda e: e.activation(gl[k][:, :], bank[bk][:, :], ACT.Gelu_apprx_tanh,
                                                      bias=b1m[:, m:m + 1]), t, R.get(("gl", k)))
                    bank_read[bk] = t
                    th = act.do(lambda e: e.activation(gh[k][0][:, :], gl[k][:, :], ACT.Copy), t, R.get(("gh", k)))
                    tl = dve.do(lambda e: e.tensor_tensor(gh[k][1][:, :], gl[k][:, :], gh[k][0][:, :], ALU.subtract),
                                th, R.get(("gh", k)))
                    R["gl", k], R["up", m] = tl, tl

                def mlp_down(m):
                    k = m % 2

                    def mm(e):
                        for b in range(NB):
                            r = product(e, bank[2 + b][:, :], [x[:, b * P:(b + 1) * P] for x in gh[k]],
                                        (w2[0][:, m, :], w2[1][:, m, :]), m == 0, m == NM - 1)
                        return r
                    t = pe.do(mm, R["up", m], w2_ready[m], bank_read[2:6] if m == 0 else None)
                    R["gh", k], R["down"] = t, t

                def x2(t):
                    z, ends = Z[t % 2], []
                    for b in range(NB):
                        q = dve.do(lambda e, b=b: e.tensor_tensor(z[:, b, :], bank[2 + b][:, :], z[:, b, :], ALU.add),
                                   R["down"], R["sb", t])
                        bank_read[2 + b] = q
                        ends.append(q)
                    R["x2", t] = ends

                def ffn(t):
                    z = Z[t % 2]
                    tn = yield from layernorm(z, stats, mv, rs, nm, R["x2", t], R.get("xn"))
                    R["xn"] = xn = []
                    xb = []
                    for b in range(NB):
                        xn.append(apply_norm_block(H, z, rs, nm, b, tn, [R["hturn"], R.get("xturn"), R.get("x1z")]))
                        xb.append(pool.do(lambda e, b=b: e.tensor_tensor(z[:, b, :], z[:, b, :], boutb[:, :],
                                                                         ALU.add), xn[-1]))
                        if b == 1:
                            yield
                    yield
                    for f in range(NF):
                        bk = 6 + f % 2
                        R["xturn"] = m = turn(H, f, bk, xn)
                        R["xT"] = bank_read[bk] = act.do(lambda e, f=f, bk=bk: e.activation(
                            xT[:, f, :], bank[bk][:, :], ACT.Copy), m, R.get(("win", 0)))
                        if f % 2:
                            yield
                    yield from hidden(xT, R["xT"], 6, relu, g, R.get("wout"), R, 0, pace=4)
                    ends = []
                    for b in range(NB):
                        bk = 6 + b % 2
                        R["wout"] = m = pe.do(lambda e, b=b, bk=bk: e.matmul(
                            bank[bk][:, :], g[:, b * P:(b + 1) * P], wout[:, :], start=True, stop=True),
                            R["g", 0], bank_read[bk])
                        q = dve.do(lambda e, b=b, bk=bk: e.tensor_tensor(z[:, b, :], bank[bk][:, :], z[:, b, :],
                                                                         ALU.add), m, xb)
                        bank_read[bk] = q
                        ends.append(q)
                        if b % 2:
                            yield
                    R["out", t] = sp.dma(d_out[t % 2], out_v[t], z[:, :, :], ends)

                def finish(*chains):
                    for c in chains:
                        for _ in c:
                            pass

                finish(rms(0))
                for f in range(NF):
                    turn_h(f)
                stage = [xT[:, f, :] for f in range(NF)] + [Z[1][:, b, :] for b in range(NB)]
                d_st3 = [box(f"d_st3{i}") for i in range(len(stage))]
                pieces = []
                for n in range(4):
                    c = slice(n * D, (n + 1) * D)
                    pieces += [(a["L0_attn_w1"][k * P:(k + 1) * P, c], w1[0][:, k, c], w1[1][:, k, c])
                               for k in range(NF)]
                pieces += [(a["L0_attn_w2"][m * P:(m + 1) * P, :], w2[0][:, m, :], w2[1][:, m, :])
                           for m in range(NM)]
                split = load_split(pieces, stage, d_st3)
                w1_ready, w2_ready = [split[4 * n:4 * n + 4] for n in range(4)], split[16:]
                R["out", -1] = R["win", 0] = split[-8:]
                for t in range(NT):
                    after = ffn(t - 1) if t else iter(())
                    left = [after]
                    for m in range(NM):
                        mlp_up(m)
                        if m == NM - 1 and t + 1 < NT:
                            finish(*left, ahead)
                            turn_h(0)
                            turn_h(1)
                        if m:
                            mlp_down(m - 1)
                        if m == 6:
                            left.append(residual(t))
                        for chain in left:
                            next(chain, 0)
                        if m == 10 and t + 1 < NT:
                            finish(*left)
                            R["z", t + 1] = load_z(t + 1)
                            ahead = rms(t + 1)
                        if m >= 13 and t + 1 < NT:
                            next(ahead, 0)
                    if t + 1 < NT:
                        turn_h(2)
                        turn_h(3)
                    else:
                        finish(*left)
                    mlp_down(NM - 1)
                    x2(t)
                finish(ffn(NT - 1))
                return [R["out", NT - 2], R["out", NT - 1]]

        stored3 = dense()
        sp.wait(stored1, stored2, stored3)

        block = top.enter_context(nc.Block())

        @block.sync
        def _(eng):
            sp.run(eng)

        @block.scalar
        def _(eng):
            act.run(eng)

        @block.vector
        def _(eng):
            dve.run(eng)

        @block.gpsimd
        def _(eng):
            pool.run(eng)

        @block.tensor
        def _(eng):
            pe.run(eng)


_INS = ['L0_attn_x', 'L0_attn_wq', 'L0_attn_bq', 'L0_attn_wk', 'L0_attn_bk', 'L0_attn_wv', 'L0_attn_bv',
        'L0_attn_wbeta', 'L0_attn_bbeta', 'L0_attn_wo', 'L0_attn_bo', 'L0_attn_w1', 'L0_attn_b1', 'L0_attn_w2',
        'L0_attn_b2', 'L0_attn_ln1_scale', 'L0_attn_ln2_scale', 'L0_ffn_Win', 'L0_ffn_bin_', 'L0_ffn_W1',
        'L0_ffn_b1', 'L0_ffn_W2', 'L0_ffn_b2', 'L0_ffn_Wout', 'L0_ffn_bout']


def kernel(**inputs):
    import numpy as _np
    import concourse.bacc as _bacc
    from concourse import mybir as _mybir
    from concourse.bass_utils import run_bass_kernel_spmd as _run

    nc = _bacc.Bacc("TRN2", target_bir_lowering=False, num_devices=1)
    f32 = _mybir.dt.float32
    arrays, args = {}, {}
    for name in _INS:
        v = _np.ascontiguousarray(inputs[name])
        arrays[f"in_{name}"] = v
        args[name] = nc.dram_tensor(f"in_{name}", v.shape, _mybir.dt.from_np(v.dtype), kind="ExternalInput").ap()
    arrays["consts"] = shape_constants()
    consts = nc.dram_tensor("consts", arrays["consts"].shape, f32, kind="ExternalInput").ap()
    shape = inputs['L0_attn_x'].shape
    T = shape[1]
    out = nc.dram_tensor("out", shape, f32, kind="ExternalOutput").ap()
    x1_d = nc.dram_tensor("x1_scratch", (T, D), f32).ap()
    z_d = nc.dram_tensor("z_scratch", (T, D), f32).ap()
    heads_d = nc.dram_tensor("heads_scratch", (T // TOK, P, 4, TU, CH), f32).ap()
    beta_d = nc.dram_tensor("beta_scratch", (T // TOK, P, TC, GROUPS), f32).ap()
    lt_d = nc.dram_tensor("lt_scratch", (T // SUP, P, GROUPS, NC, CH), f32).ap()
    macaron(nc, args, consts, out, x1_d, z_d, heads_d, beta_d, lt_d)
    r = _run(nc, [arrays], core_ids=[0])
    return r.results[0]["out"]
```
